# Optimizing a Trainium2 kernel written in Bass

```python
import numpy as np
import jax
import jax.numpy as jnp

def _softmax(x, axis=-1):
    return jax.nn.softmax(x, axis=axis)

def _gelu(x):
    return jax.nn.gelu(x, approximate=True)

def _silu(x):
    return jax.nn.silu(x)

def _sigmoid(x):
    return jax.nn.sigmoid(x)

def _layernorm(x, axis=-1, eps=1e-05):
    m = jnp.mean(x, axis=axis, keepdims=True)
    v = jnp.var(x, axis=axis, keepdims=True)
    return (x - m) / jnp.sqrt(v + eps)

def _scatter_add(tgt, idx, src, axis=0):
    return tgt.at[idx].add(src)

def _segment_sum(src, seg, n):
    return jax.ops.segment_sum(src, seg, n)
kernel_name = 'mk_adaln_d1_jaxref_r4_a2eb44'

def setup_inputs(seed: int=0):
    np.random.seed(seed)
    _w = jnp.asarray

    def _L0_attn_setup():
        import jax, jax.numpy as jnp
        import numpy as np
        D_MODEL = 256
        N_HEADS = 16
        HEAD_DIM = D_MODEL // N_HEADS
        LORA_RANK = 16
        LORA_SCALING = 1.0 / LORA_RANK

        def lora_linear(x, w, a, b):
            return x @ w.T + LORA_SCALING * (x @ a.T @ b.T)
        key = jax.random.key(seed)
        ks = jax.random.split(key, 14)
        B, S = (4, 512)

        def w(k, shape, scale=0.02):
            return jax.random.normal(k, shape, dtype=jnp.float32) * scale
        inp = {'x': jax.random.normal(ks[0], (B, S, D_MODEL), dtype=jnp.float32), 'wq': w(ks[1], (D_MODEL, D_MODEL)), 'aq': w(ks[2], (LORA_RANK, D_MODEL)), 'bq': w(ks[3], (D_MODEL, LORA_RANK)), 'wk': w(ks[4], (D_MODEL, D_MODEL)), 'ak': w(ks[5], (LORA_RANK, D_MODEL)), 'bk': w(ks[6], (D_MODEL, LORA_RANK)), 'wv': w(ks[7], (D_MODEL, D_MODEL)), 'av': w(ks[8], (LORA_RANK, D_MODEL)), 'bv': w(ks[9], (D_MODEL, LORA_RANK)), 'wo': w(ks[10], (D_MODEL, D_MODEL)), 'ao': w(ks[11], (LORA_RANK, D_MODEL)), 'bo': w(ks[12], (D_MODEL, LORA_RANK))}
        return inp
    _L0_attn_in = _L0_attn_setup()

    def _L0_ffn_setup():
        import jax, jax.numpy as jnp
        import numpy as np
        TOP_K = 2
        key = jax.random.key(seed)
        ks = jax.random.split(key, 7)
        B_, S, D, F, E, R = (2, 512, 256, 1024, 4, 4)
        x = jax.random.normal(ks[0], (B_, S, D), dtype=jnp.float32)
        Wg = jax.random.normal(ks[1], (E, D), dtype=jnp.float32) * (1.0 / np.sqrt(D))
        bg = jnp.zeros((E,), dtype=jnp.float32)
        Wi = jax.random.normal(ks[2], (F, D), dtype=jnp.float32) * (1.0 / np.sqrt(D))
        Wo = jax.random.normal(ks[3], (D, F), dtype=jnp.float32) * (1.0 / np.sqrt(F))
        A = jax.random.normal(ks[4], (E, R, D), dtype=jnp.float32) * (1.0 / np.sqrt(D))
        Bm = jax.random.normal(ks[5], (E, F, R), dtype=jnp.float32) * 0.01
        return {'x': x, 'Wg': Wg, 'bg': bg, 'Wi': Wi, 'Wo': Wo, 'A': A, 'B': Bm}
    _L0_ffn_in = _L0_ffn_setup()
    _L0_c = _w((lambda *s: np.random.randn(*s).astype(np.float32) * 0.05)(8, 256))
    _L0_wmod = _w((lambda *s: np.random.randn(*s).astype(np.float32) * 0.05)(256, 6 * 256) * 256 ** (-0.5))
    _d = {'L0_attn_x': _L0_attn_in['x'], 'L0_attn_wq': _L0_attn_in['wq'], 'L0_attn_aq': _L0_attn_in['aq'], 'L0_attn_bq': _L0_attn_in['bq'], 'L0_attn_wk': _L0_attn_in['wk'], 'L0_attn_ak': _L0_attn_in['ak'], 'L0_attn_bk': _L0_attn_in['bk'], 'L0_attn_wv': _L0_attn_in['wv'], 'L0_attn_av': _L0_attn_in['av'], 'L0_attn_bv': _L0_attn_in['bv'], 'L0_attn_wo': _L0_attn_in['wo'], 'L0_attn_ao': _L0_attn_in['ao'], 'L0_attn_bo': _L0_attn_in['bo'], 'L0_ffn_Wg': _L0_ffn_in['Wg'], 'L0_ffn_bg': _L0_ffn_in['bg'], 'L0_ffn_Wi': _L0_ffn_in['Wi'], 'L0_ffn_Wo': _L0_ffn_in['Wo'], 'L0_ffn_A': _L0_ffn_in['A'], 'L0_ffn_B': _L0_ffn_in['B'], 'L0_c': _L0_c, 'L0_wmod': _L0_wmod}
    _x0 = _d['L0_attn_x']
    _d['L0_attn_x'] = jax.random.normal(jax.random.fold_in(jax.random.key(seed), 1), (8, 1024, 256), dtype=_x0.dtype)
    del _x0
    return _d

def reference(L0_attn_x, L0_attn_wq, L0_attn_aq, L0_attn_bq, L0_attn_wk, L0_attn_ak, L0_attn_bk, L0_attn_wv, L0_attn_av, L0_attn_bv, L0_attn_wo, L0_attn_ao, L0_attn_bo, L0_ffn_Wg, L0_ffn_bg, L0_ffn_Wi, L0_ffn_Wo, L0_ffn_A, L0_ffn_B, L0_c, L0_wmod):

    def _L0_attn_ref(x, wq, aq, bq, wk, ak, bk, wv, av, bv, wo, ao, bo):
        import jax, jax.numpy as jnp
        import numpy as np
        D_MODEL = 256
        N_HEADS = 16
        HEAD_DIM = D_MODEL // N_HEADS
        LORA_RANK = 16
        LORA_SCALING = 1.0 / LORA_RANK

        def lora_linear(x, w, a, b):
            return x @ w.T + LORA_SCALING * (x @ a.T @ b.T)
        B, S, _ = x.shape

        def split_heads(t):
            return t.reshape(B, S, N_HEADS, HEAD_DIM).transpose(0, 2, 1, 3)
        q = split_heads(lora_linear(x, wq, aq, bq))
        k = split_heads(lora_linear(x, wk, ak, bk))
        v = split_heads(lora_linear(x, wv, av, bv))
        scores = jnp.einsum('bhqd,bhkd->bhqk', q, k) / jnp.sqrt(jnp.float32(HEAD_DIM))
        causal = jnp.tril(jnp.ones((S, S), dtype=bool))
        scores = jnp.where(causal, scores, -jnp.inf)
        attn = jax.nn.softmax(scores, axis=-1)
        ctx = jnp.einsum('bhqk,bhkd->bhqd', attn, v)
        ctx = ctx.transpose(0, 2, 1, 3).reshape(B, S, D_MODEL)
        return lora_linear(ctx, wo, ao, bo)

    def _L0_ffn_ref(x, Wg, bg, Wi, Wo, A, B):
        import jax, jax.numpy as jnp
        import numpy as np
        TOP_K = 2
        E = Wg.shape[0]
        logits = jnp.einsum('bsd,ed->bse', x, Wg) + bg
        scores = jax.nn.softmax(logits, axis=-1)
        topv, topi = jax.lax.top_k(scores, TOP_K)
        w = jnp.sum(jax.nn.one_hot(topi, E, dtype=x.dtype) * topv[..., None], axis=-2)
        base = jnp.einsum('bsd,fd->bsf', x, Wi)
        lora_low = jnp.einsum('bsd,erd->bser', x, A)
        lora = jnp.einsum('bser,efr->bsef', lora_low, B)
        h = jax.nn.relu(base[:, :, None, :] + lora)
        expert_out = jnp.einsum('bsef,df->bsed', h, Wo)
        out = jnp.einsum('bse,bsed->bsd', w, expert_out)
        return out
    x = L0_attn_x
    mod = (_silu(L0_c) @ L0_wmod).reshape(L0_c.shape[0], 6, 1, -1)
    sa, ca, ga, sb, cb, gb = (mod[:, 0], mod[:, 1], mod[:, 2], mod[:, 3], mod[:, 4], mod[:, 5])
    ga = (2 * (ga >= 0) - 1) * jnp.maximum(jnp.abs(ga), 0.25)
    gb = (2 * (gb >= 0) - 1) * jnp.maximum(jnp.abs(gb), 0.25)
    h = _layernorm(x, axis=-1) * (1 + ca) + sa
    x = x + ga * _L0_attn_ref(h, L0_attn_wq, L0_attn_aq, L0_attn_bq, L0_attn_wk, L0_attn_ak, L0_attn_bk, L0_attn_wv, L0_attn_av, L0_attn_bv, L0_attn_wo, L0_attn_ao, L0_attn_bo)
    h = _layernorm(x, axis=-1) * (1 + cb) + sb
    x = x + gb * _L0_ffn_ref(h, L0_ffn_Wg, L0_ffn_bg, L0_ffn_Wi, L0_ffn_Wo, L0_ffn_A, L0_ffn_B)
    return x

_drawn_inputs = setup_inputs


def setup_inputs(seed=0):
    import zlib

    import numpy as np

    out = dict(_drawn_inputs(seed))
    spreads = {'L0_ffn_bg': (0.0, 0.8)}
    factors = {'L0_attn_wq': 8.0,
     'L0_attn_aq': 8.0,
     'L0_attn_bq': 8.0,
     'L0_attn_wk': 8.0,
     'L0_attn_ak': 8.0,
     'L0_attn_bk': 8.0,
     'L0_attn_wv': 8.0,
     'L0_attn_av': 8.0,
     'L0_attn_bv': 8.0,
     'L0_attn_wo': 8.0,
     'L0_attn_ao': 8.0,
     'L0_attn_bo': 8.0,
     'L0_ffn_Wg': 3.341,
     'L0_ffn_A': 8.0,
     'L0_ffn_B': 8.0}
    for name, (base, spread) in spreads.items():
        noise = np.random.default_rng([zlib.crc32(name.encode()), seed]).standard_normal(out[name].shape)
        drawn = base * np.exp(spread * noise) if base else spread * noise
        out[name] = jnp.asarray(drawn.astype(out[name].dtype))
    for name, factor in factors.items():
        out[name] = (out[name] * factor).astype(out[name].dtype)
    return out
```

```python
from contextlib import ExitStack

import concourse.bass as bass
from concourse import mybir

F32 = mybir.dt.float32
BF16 = mybir.dt.bfloat16
I32 = mybir.dt.int32
ALU = mybir.AluOpType
ACT = mybir.ActivationFunctionType
AX = mybir.AxisListType

P = 128
DH = 16
HG = 4
SPLIT = 6
Q_PARTS = (0, 0, 1, 1, 0, 2)
K_PARTS = (0, 1, 0, 1, 2, 0)
KS = SPLIT * DH
BIG = -3.0e38
LN_EPS = 1e-5
RSQRT_SEED = float(0x5F3759DF)
GATE_MIN = 0.25

DENSE = frozenset("su t1 pj vp ct op t2 rt rx mt rb fa fb w ce nm".split())


def attention_units():
    return [(c, kt) for c in range(2) for kt in range(4 * (c + 1))]


UNITS = attention_units()
NU = len(UNITS)
GROUPS = 4


def max_steps():
    return [(p, jj, qt) for p in range(2)
            for jj, qt in [(jj, qt) for qt in range(7, 3, -1) for jj in range(2)]
            + [(None, qt) for qt in range(3, -1, -1)]]


def pe_cost(step):
    return {"ct": 300, "op": 1750, "t1": 300, "t2": 300, "rt": 1000, "rx": 200, "mt": 500, "rb": 300,
            "pj": 1750, "vp": 1750, "fa": 1950, "fb": 250, "w": 3500, "ce": 300, "nm": 500}.get(step[0], 0)


def body_plan(pre, post, lead):
    queue = []

    def put(unit, *steps):
        queue.extend((unit, (s,)) for s in steps)

    if post:
        put(0, ("ce", GROUPS - 1, 1))
        put(1, *[("ct", i) for i in range(4)], *[("op", i) for i in range(4)], ("ln2",))
    if pre:
        put(3, ("ln1",))
        put(4, *[("t1", i) for i in range(4)])
    if post:
        put(5, *[("t2", i) for i in range(4)], ("rt",), ("rx",), ("ro",))
    if pre:
        put(9, *[("pj", w, 0, half) for half in range(2) for w in "qk"], ("ps", 0))
    late = [(33, (("vp", i),)) for i in range(4)]
    late += [(24, (("pj", w, 1, half),)) for half in range(2) for w in "qk"] + [(24, (("ps", 1),))]
    if post:
        put(9, *[("mt", v) for v in range(2)], *[("rb", half) for half in range(2)])
        for half in range(2):
            for ft in range(8):
                queue.append((9, (("fa", half, ft), ("fb", half, ft))))
                if half and ft % 2 and pre:
                    queue += [late.pop(0), late.pop(0)]
            if half and pre:
                queue += late
            put(9, *[("w", half, t) for t in range(4)])
    elif pre:
        queue += late
    unit_cost = [8 * 512 / 2.4 if kt < 4 * c else 8 * (512 - 128 * (kt % 4)) / 2.4 for c, kt in UNITS]
    maxes = [0, 0, 0, 2, 3, 3, 4, 4, 4, 4, 0, 0]
    total = (sum(unit_cost) + 24 * 400) * GROUPS + sum(pe_cost(s) for _, q in queue for s in q) + 8 * 300 + 4 * 500
    spent = 0.0
    plan = []
    if post:
        plan.append(("xl",))
    if pre:
        plan.append(("xin",))
    for u in range(GROUPS * NU):
        g, k = divmod(u, NU)
        c, kt = UNITS[k]
        more = lead or g < GROUPS - 1
        fillers = []
        if k == NU - 2 and more:
            fillers.append(("nm", (g + 1) % 2))
        if k in (4, 0) and not (k == 0 and g == 0):
            fillers.append(("ce", g, 0) if k == 4 else ("ce", g - 1, 1))
        spent += unit_cost[k] + maxes[k] * 400 * more + sum(pe_cost(s) for s in fillers)
        goal = total * (u + 1) / (GROUPS * NU)
        while queue and queue[0][0] <= u and (spent + sum(map(pe_cost, queue[0][1])) / 2 <= goal or u == GROUPS * NU - 1):
            fillers += queue[0][1]
            spent += sum(map(pe_cost, queue.pop(0)[1]))
        mx = [("mx", (g + 1) % 2, *s) for s in max_steps()[sum(maxes[:k]):sum(maxes[:k + 1])]] if more else []
        following = [("qk", (u + 1) // NU % 2, *UNITS[(u + 1) % NU])] if u + 1 < GROUPS * NU or lead else []
        if k == NU - 1 and (pre or g < 2):
            plan.append(("rs", g % 2, (g + 2) % GROUPS))
        if k < NU - 1:
            plan += following
        while mx or fillers:
            if fillers:
                plan.append(fillers.pop(0))
            if mx:
                plan.append(mx.pop(0))
        if k == 9 and more:
            plan.append(("ms",))
        plan.append(("pv", g % 2, c, kt))
        if kt == 4 * c + 3:
            plan.append(("ov", c))
        if k == NU - 1:
            plan += following
        if k == 8 and more:
            plan.append(("vg", (g + 1) % GROUPS))
    assert not queue
    return plan


def prologue_plan():
    plan = [("su", i) for i in range(N_SETUP)]
    plan += [("ln1",)] + [("t1", i) for i in range(4)]
    for ot in range(2):
        plan += [("pj", w, ot, half) for half in range(2) for w in "qk"] + [("ps", ot)]
    plan += [("vp", i) for i in range(4)]
    plan += [("rs", 0, 0), ("rs", 1, 1), ("vg", 0)]
    plan += [("mx", 0, *s) for s in max_steps()] + [("ms",), ("nm", 0), ("qk", 0, *UNITS[0])]
    return plan


def epilogue_plan():
    plan = [("xl",), ("ce", GROUPS - 1, 1)] + [("ct", i) for i in range(4)] + [("op", i) for i in range(4)]
    plan += [("ln2",)] + [("t2", i) for i in range(4)] + [("rt",), ("rx",), ("ro",)]
    plan += [("mt", v) for v in range(2)] + [("rb", half) for half in range(2)]
    for half in range(2):
        for ft in range(8):
            plan += [("fa", half, ft), ("fb", half, ft)]
        plan += [("w", half, t) for t in range(4)]
    return plan


N_SETUP = 20


def tallied(step):
    names = [step[0]]
    if step[0] in DENSE:
        names.append("dense")
    if step[0] in ("qk", "pv") and step[2] == step[3] // 4:
        names.append(step[0] + " diagonal")
    if step[0] in ("rs", "ps"):
        names.append(f"{step[0]}{step[1]}")
    if step[0] == "w":
        names.append(f"w{step[2] % 2}")
    return names


def walk(eng, batches, run):
    counts = {}

    def phase(plan, it, reg):
        per = {}
        for s in plan:
            for n in tallied(s):
                per[n] = per.get(n, 0) + 1
        here = {}
        for s in plan:
            def done(name, here=dict(here)):
                fixed = counts.get(name, 0) + here.get(name, 0)
                return fixed if reg is None or not per.get(name) else reg * per[name] + fixed
            run(s, done, it)
            for n in tallied(s):
                here[n] = here.get(n, 0) + 1
        for n, m in per.items():
            counts[n] = counts.get(n, 0) + m * (1 if reg is None else batches - 2)

    phase(prologue_plan(), -1, None)
    phase(body_plan(pre=True, post=False, lead=True), 0, None)
    with eng.Fori(0, batches - 2) as reg:
        phase(body_plan(pre=True, post=True, lead=True), reg + 1, reg)
    phase(body_plan(pre=False, post=True, lead=False), batches - 1, None)
    phase(epilogue_plan(), batches, None)


def after(eng, sem, value):
    if not isinstance(value, int) or value > 0:
        eng.wait_ge(sem, value)


def held(eng, value):
    return value if isinstance(value, int) else eng.to_reg(value)


def adaln_block(nc, x, wq, aq, bq, wk, ak, bk, wv, av, bv, wo, ao, bo, Wg, bg, Wi, Wo, A, Bm, c, wmod, out):
    NB, S, D = x.shape
    R = aq.shape[0]
    F = Wi.shape[0]
    E, RK, _ = A.shape
    T = S // P
    KC = D // P
    FT = F // P
    HB = S // 2
    LORA_SCALE = 1.0 / R
    SCORE_SCALE = float(DH) ** -0.5
    assert (S, D, R, F, E * RK, NB) == (1024, 256, DH, 1024, DH, 8)

    x_t = x.rearrange("b (t p) d -> b p t d", p=P)
    out_t = out.rearrange("b (t p) d -> b t p d", p=P)

    with ExitStack() as ctx:
        def sb(name, shape, dt=F32):
            return ctx.enter_context(nc.sbuf_tensor(name, shape, dt))

        def sem(name):
            return ctx.enter_context(nc.semaphore(name))

        ident = sb("ident", [P, P])
        ident_b = sb("ident_b", [P, P], BF16)
        causal_b = sb("causal_b", [P, P], BF16)
        w_t = sb("w_t", [P, 4, KC, D])
        wi_t = sb("wi_t", [P, KC, F])
        wo_t = sb("wo_t", [P, FT, D])
        rout_t = sb("rout_t", [P, KC, 32])
        b_stack = sb("b_stack", [P, F], BF16)
        bg_b = sb("bg_b", [P, E])
        prio = sb("prio", [P, T, E])
        mod_t = sb("mod_t", [P, NB, 8])
        mod1 = sb("mod1", [P, 4])
        mod2 = sb("mod2", [P, 4])
        gates_b = sb("gates_b", [P, 2 * D])
        xin = sb("xin", [P, T, D])
        x1 = sb("x1", [P, T, D])
        h_t = sb("h_t", [P, KC, S])
        ctx_n = sb("ctx_n", [P, T, D])
        c_t = sb("c_t", [P, KC, S])
        v_st = sb("v_st", [P, T, D])
        v_g = sb("v_g", [P, 2, T, HG, 32])
        q_part = sb("q_part", [P, 2, 3, S], BF16)
        k_part = sb("k_part", [P, 2, 3, S], BF16)
        rest = sb("rest", [P, 2, HB])
        q_st = sb("q_st", [P, 2, HG, S], BF16)
        k_st = sb("k_st", [P, 2, HG, S], BF16)
        probs = sb("probs", [P, 2, 2, 2, HB])
        o_sb = sb("o_sb", [P, 2, HB])
        hid = sb("hid", [P, FT, HB])
        second = sb("second", [P, 2, HB])
        ob = sb("ob", [P, 2, D])
        ratio_b = sb("ratio_b", [P, 2, HB])
        low_st = sb("low_st", [P, 2, S], BF16)
        low_w = sb("low_w", [P, 2, T, SPLIT, DH], BF16)
        rout_sb = sb("rout_sb", [P, D])
        m_row = sb("m_row", [8, S], BF16)
        negm = sb("negm", [P, T, HG])
        m_w = sb("m_w", [P, T, HG, 2], BF16)
        rsum = sb("rsum", [P, 4, HG])
        stats = sb("stats", [P, T, 6])
        fence = sb("fence", [P, 4])
        mv = sb("mv", [P, T, 2])
        nt = sb("nt", [P, 4, T])
        lg = sb("lg", [P, T, E + DH])
        rv = sb("rv", [P, 8, T, E])
        rs_ = sb("rs_", [P, 8, T])
        lowf = sb("lowf", [P, 2, T, DH])
        lowr = sb("lowr", [P, 2, T, DH])
        ratio_w = second[:, :, :].rearrange("p a (t n) -> p (a t) n", n=P)
        x2n = hid[:, :, :].rearrange("p a b -> p (a b)")[:, 0:T * D].rearrange("p (t d) -> p t d", t=T)

        hid_f = hid[:, :, :].rearrange("p a b -> p (a b)")
        wi_raw = hid_f[:, 0:FT * D].rearrange("p (t d) -> p t d", t=FT)
        wo_raw = hid_f[:, FT * D:2 * FT * D].rearrange("p (t f) -> p t f", t=KC)
        probs_f = probs[:, :, :, :, :].rearrange("p a b c d -> p (a b c d)")
        wmod_sb = probs_f[:, 0:KC * 6 * D].rearrange("p (k n) -> p k n", k=KC)
        a_pad = probs_f[:, KC * 6 * D:KC * 6 * D + 4 * D].rearrange("p (m d) -> p m d", m=4)
        qp_f = q_part[:, :, :, :].rearrange("p a b c -> p (a b c)").bitcast(F32)
        w_raw = qp_f[:, 0:4 * KC * D].rearrange("p (m t d) -> p m t d", m=4, t=KC)
        bt_pad = qp_f[:, 2048:2048 + 4 * D].rearrange("p (m d) -> p m d", m=4)
        kp_f = k_part[:, :, :, :].rearrange("p a b c -> p (a b c)").bitcast(F32)
        b_raw = kp_f[:, 0:128].rearrange("p (m t r) -> p m t r", m=4, t=KC)
        eb_raw = kp_f[:, 128:256].rearrange("p (t n) -> p t n", t=FT)
        eb_rest = kp_f[:, 256:384].rearrange("p (t n) -> p t n", t=FT)
        eb_w = k_part[:, 0, 1, 0:FT * KS].rearrange("p (t s n) -> p t s n", t=FT, s=SPLIT)
        r_raw = kp_f[:, 1024:1280]
        c_raw = kp_f[:, 1280:1536]
        c_sig = kp_f[:, 1536:1792]
        c_sil = kp_f[:, 1792:2048]
        cond_t = kp_f[:, 2048:2048 + KC * NB].rearrange("p (k b) -> p k b", k=KC)
        gate_raw = kp_f[:, 2304:2304 + 2 * D]
        gate_abs = o_sb[:, 0, :]
        gate_sgn = o_sb[:, 1, :]

        st = ctx.enter_context(nc.psum_tensor("st", [P, 2, 2, HB], F32))
        ov = ctx.enter_context(nc.psum_tensor("ov", [P, HB], F32))
        mxs = ctx.enter_context(nc.psum_tensor("mxs", [P, 2 * HB], F32))
        db = ctx.enter_context(nc.psum_tensor("db", [P, HB], F32))
        db_b = db[:, :].bitcast(BF16)

        q_d, k_d = (nc.dram_tensor(f"{w}_parts_scratch", [2, P, 3, S], BF16, kind="Internal").ap() for w in "qk")
        gates_d = nc.dram_tensor("gates_scratch", [NB, 2 * D], F32, kind="Internal").ap()

        weights_in = sem("weights_in")
        cond_in = sem("cond_in")
        wmod_in = sem("wmod_in")
        expert_in = sem("expert_in")
        zeroed = sem("zeroed")
        consts_ready = sem("consts_ready")
        gates_out = sem("gates_out")
        setup_chain = sem("setup_chain")
        cond_exp = sem("cond_exp")
        xin_in = sem("xin_in")
        x1_in = sem("x1_in")
        gates_in = sem("gates_in")
        norm1_ready = sem("norm1_ready")
        norm2_ready = sem("norm2_ready")
        norm_chain = sem("norm_chain")
        dense_full = sem("dense_full")
        dense_free = sem("dense_free")
        part1_ready = sem("part1_ready")
        rest_ready = sem("rest_ready")
        part2_ready = sem("part2_ready")
        part3_ready = sem("part3_ready")
        stack_in = [sem(f"stack_in{s}") for s in range(2)]
        parts_out = [sem(f"parts_out{i}") for i in range(2)]
        max_full = sem("max_full")
        max_free = sem("max_free")
        negm_split = sem("negm_split")
        negm_hi = sem("negm_hi")
        m_row_in = sem("m_row_in")
        scores_ready = sem("scores_ready")
        exp_done = sem("exp_done")
        fenced = sem("fenced")
        masked = sem("masked")
        vg_ready = sem("vg_ready")
        pv_done = sem("pv_done")
        ov_free = sem("ov_free")
        rsum_ready = sem("rsum_ready")
        x1_ready = sem("x1_ready")
        route_chain = sem("route_chain")
        route_diff = sem("route_diff")
        route_exp = sem("route_exp")
        route_ready = sem("route_ready")
        hid_ready = sem("hid_ready")
        out_scaled = sem("out_scaled")
        out_ready = sem("out_ready")
        out_done = [sem(f"out_done{i}") for i in range(2)]

        WNAMES = "qkvo"
        W_IN = 16 * 16
        NORM_LINKS = 2 * T + 1 + 2 + 3 * 3
        ROUTE_LINKS = 23

        block = ctx.enter_context(nc.Block())

        @block.sync
        def _(sp):
            sp.wait_ge(zeroed, 2)
            sp.dma_start(c_raw[0:NB, :], c).then_inc(cond_in, 16)
            sp.dma_start(xin[:, :, :], x_t[0]).then_inc(xin_in, 16)
            sp.dma_start(wmod_sb, wmod.rearrange("(k p) n -> p k n", p=P)).then_inc(wmod_in, 16)
            for m, (w, a, b) in enumerate(((wq, aq, bq), (wk, ak, bk), (wv, av, bv), (wo, ao, bo))):
                sp.dma_start(w_raw[:, m], w.rearrange("(t p) d -> p t d", p=P)).then_inc(weights_in, 16)
                sp.dma_start(a_pad[0:R, m], a).then_inc(weights_in, 16)
                sp.dma_start(b_raw[:, m], b.rearrange("(t p) r -> p t r", p=P)).then_inc(weights_in, 16)
            sp.dma_start(r_raw[0:E, :], Wg).then_inc(weights_in, 16)
            sp.dma_start(r_raw[E:E + DH, :], A.rearrange("e r d -> (e r) d")).then_inc(expert_in, 16)
            sp.dma_start(wi_raw, Wi.rearrange("(t p) d -> p t d", p=P)).then_inc(weights_in, 16)
            sp.dma_start(wo_raw, Wo.rearrange("(t p) f -> p t f", p=P)).then_inc(weights_in, 16)
            for e in range(E):
                sp.dma_start(eb_raw[:, :, e * RK:(e + 1) * RK],
                             Bm[e].rearrange("(t p) r -> p t r", p=P)).then_inc(expert_in, 16)
            sp.dma_start(bg_b[:, :], bg.partition_broadcast(P)).then_inc(weights_in, 16)

            def run(step, done, it):
                kind, *a = step
                if kind == "xin":
                    after(sp, dense_full, done("dense"))
                    sp.dma_start(xin[:, :, :], x_t[it + 1]).then_inc(xin_in, 16)
                elif kind == "xl":
                    after(sp, out_ready, done("w"))
                    sp.dma_start(x1[:, :, :], x_t[it - 1]).then_inc(x1_in, 16)
                    sp.wait_ge(gates_out, 16)
                    sp.dma_start(gates_b[:, :], gates_d[it - 1].partition_broadcast(P)).then_inc(gates_in, 16)
                elif kind == "ps":
                    ot = a[0]
                    stacked = [held(sp, done(f"rs{s}") * (2 * SPLIT * 16)) for s in range(2)]
                    split = held(sp, done("pj"))
                    sp.wait_ge(part3_ready, split)
                    for s in range(2):
                        after(sp, stack_in[s], stacked[s])
                    for dst, src in ((q_d, q_part), (k_d, k_part)):
                        sp.dma_start(dst[ot], src[:, ot, :, :]).then_inc(parts_out[ot], 16)
                elif kind == "rs":
                    slot, g = a
                    ot, lower = divmod(g, 2)
                    scored, stored = held(sp, 2 * done("qk")), held(sp, done(f"ps{ot}") * (2 * 16))
                    after(sp, scores_ready, scored)
                    sp.wait_ge(parts_out[ot], stored)
                    rows = slice(lower * HG * DH, (lower + 1) * HG * DH)
                    for s in range(SPLIT):
                        for dst, src, part in ((q_st, q_d, Q_PARTS[s]), (k_st, k_d, K_PARTS[s])):
                            heads = src[ot, rows, part, :].rearrange("(j d) n -> d j n", j=HG)
                            sp.dma_start(dst[s * DH:(s + 1) * DH, slot, :, :], heads).then_inc(stack_in[slot], 16)
                elif kind == "w":
                    half, t = a
                    sp.wait_ge(out_ready, done("w") + 1)
                    sp.dma_start(out_t[it - 1, 4 * half + t], ob[:, t % 2, :]).then_inc(out_done[t % 2], 16)

            walk(sp, NB, run)
            for s in out_done:
                sp.wait_ge(s, 16 * NB * T // 2)

        @block.gpsimd
        def _(pool):
            nc.gpsimd.memset(fence[:, 0:3], 0.0).then_inc(consts_ready, 1)
            nc.gpsimd.memset(a_pad, 0.0).then_inc(zeroed, 1)
            nc.gpsimd.memset(r_raw[0:32, :], 0.0).then_inc(zeroed, 1)
            nc.gpsimd.memset(bt_pad, 0.0).then_inc(zeroed, 1)
            nc.gpsimd.memset(ident[:, :], 0.0).then_inc(zeroed, 1)
            nc.gpsimd.memset(causal_b[:, :], 0.0).then_inc(zeroed, 1)
            pool.wait_ge(zeroed, 5)
            nc.gpsimd.affine_select(out=ident[:, :], in_=ident[:, :], compare_op=ALU.not_equal, fill=1.0,
                                    base=0, pattern=[[-1, P]], channel_multiplier=1).then_inc(zeroed, 1)
            pool.wait_ge(zeroed, 6)
            nc.gpsimd.tensor_copy(ident_b[:, :], ident[:, :]).then_inc(consts_ready, 1)
            nc.gpsimd.affine_select(out=causal_b[:, :], in_=causal_b[:, :], compare_op=ALU.is_ge, fill=BIG,
                                    base=0, pattern=[[-1, P]], channel_multiplier=1).then_inc(consts_ready, 1)
            nc.gpsimd.memset(v_g[:, :, :, :, :], 0.0).then_inc(zeroed, 1)
            pool.wait_ge(zeroed, 7)
            nc.gpsimd.memset(v_g[:, :, :, :, DH:DH + 1], 1.0).then_inc(consts_ready, 1)
            for e in range(E):
                nc.gpsimd.memset(prio[:, :, e:e + 1], float(E - e)).then_inc(consts_ready, 1)

            def run(step, done, it):
                kind, *a = step
                if kind == "qk":
                    slot, ch, kt = a
                    if kt // 4 == ch:
                        par = UNITS.index((ch, kt)) % 2
                        pool.wait_ge(exp_done, 2 * done("qk") + 2)
                        after(pool, fenced, done("qk diagonal"))
                        nc.gpsimd.tensor_tensor(fence[:, 0:1], fence[:, 1:2], fence[:, 2:3],
                                                ALU.mult).then_inc(fenced, 1)
                        tri = probs[:, par, :, :, 0:P].rearrange("p a b k -> p (a b) k")
                        nc.gpsimd.affine_select(
                            out=tri, in_=tri, compare_op=ALU.is_ge, fill=0.0, base=0,
                            pattern=[[0, HG], [1, P]], channel_multiplier=-1).then_inc(masked, 1)
                elif kind == "pj":
                    which, ot, half = a
                    dst = (q_part if which == "q" else k_part)[:, ot, :, half * HB:(half + 1) * HB]
                    par = 0 if which == "q" else 1
                    pool.wait_ge(part2_ready, done("pj") + 1)
                    nc.gpsimd.tensor_tensor(dst[:, 2, :], rest[:, par, :], dst[:, 1, :],
                                            ALU.subtract).then_inc(part3_ready, 1)
                elif kind == "op":
                    i = a[0]
                    if i == 0:
                        pool.wait_ge(x1_in, 16 * (done("xl")))
                    pool.wait_ge(dense_free, done("dense") + 1)
                    nc.gpsimd.tensor_tensor(
                        x1[:, 2 * i:2 * i + 2, :], x1[:, 2 * i:2 * i + 2, :],
                        second[:, i % 2, :].rearrange("p (t d) -> p t d", t=2), ALU.add).then_inc(x1_ready, 1)
                elif kind == "fb":
                    half, ft = a
                    pool.wait_ge(dense_free, done("dense") + 1)
                    nc.gpsimd.tensor_tensor(hid[:, ft, :], hid[:, ft, :], second[:, ft % 2, :],
                                            ALU.add).then_inc(hid_ready, 1)
                elif kind == "w":
                    half, t = a
                    pool.wait_ge(dense_free, done("dense") + 1)
                    nc.gpsimd.tensor_tensor(ob[:, t % 2, :], ob[:, t % 2, :], x1[:, 4 * half + t, :],
                                            ALU.add).then_inc(out_ready, 1)

            walk(pool, NB, run)

        @block.tensor
        def _(pe):
            def setup(i):
                if i == 0:
                    pe.wait_ge(consts_ready, 9)
                    pe.wait_ge(setup_chain, 3)
                    for k in range(KC):
                        last = nc.tensor.transpose(db[:, k * NB:(k + 1) * NB], c_sil[0:NB, k * P:(k + 1) * P],
                                                   ident[0:NB, 0:NB])
                elif i == 1:
                    pe.wait_ge(wmod_in, 16)
                    for n, piece in enumerate((0, 1, 2, 3, 6, 7, 8, 9)):
                        for k in range(KC):
                            last = nc.tensor.matmul(db[:, n * NB:(n + 1) * NB],
                                                    wmod_sb[:, k, piece * P:(piece + 1) * P], cond_t[:, k, :],
                                                    start=(k == 0), stop=(k == KC - 1))
                elif i == 2:
                    for n, piece in enumerate((2, 5)):
                        for k in range(KC):
                            last = nc.tensor.matmul(db[0:NB, n * D:(n + 1) * D], cond_t[:, k, :],
                                                    wmod_sb[:, k, piece * D:(piece + 1) * D],
                                                    start=(k == 0), stop=(k == KC - 1))
                elif i <= 4:
                    pe.wait_ge(weights_in, W_IN)
                    for n in range(2):
                        for t in range(KC):
                            last = nc.tensor.matmul(db[0:R, n * D + t * P:n * D + (t + 1) * P],
                                                    b_raw[:, 2 * (i - 3) + n, t, :], ident[:, :],
                                                    start=True, stop=True)
                elif i <= 8:
                    m = i - 5
                    for k in range(KC):
                        for t in range(KC):
                            o = db[:, k * D + t * P:k * D + (t + 1) * P]
                            nc.tensor.matmul(o, w_raw[:, m, t, k * P:(k + 1) * P], ident[:, :],
                                             start=True, stop=False)
                            last = nc.tensor.matmul(o, a_pad[:, m, k * P:(k + 1) * P],
                                                    bt_pad[:, m, t * P:(t + 1) * P], start=False, stop=True)
                elif i <= 12:
                    k, half = divmod(i - 9, 2)
                    for t in range(4):
                        last = nc.tensor.transpose(db[:, t * P:(t + 1) * P],
                                                   wi_raw[:, 4 * half + t, k * P:(k + 1) * P], ident[:, :])
                elif i <= 16:
                    for n in range(2):
                        for t in range(KC):
                            ft = 2 * (i - 13) + n
                            last = nc.tensor.transpose(db[:, n * D + t * P:n * D + (t + 1) * P],
                                                       wo_raw[:, t, ft * P:(ft + 1) * P], ident[:, :])
                elif i == 17:
                    pe.wait_ge(expert_in, 16 * (1 + E))
                    for k in range(KC):
                        last = nc.tensor.transpose(db[:, k * 32:(k + 1) * 32], r_raw[0:32, k * P:(k + 1) * P],
                                                   ident[0:32, 0:32])
                elif i == 18:
                    pe.wait_ge(setup_chain, 11)
                    for t in range(FT):
                        last = nc.tensor.transpose(db_b[0:KS, t * P:(t + 1) * P],
                                                   eb_w[:, t].rearrange("p s n -> p (s n)"), ident_b[:, :])
                else:
                    last = nc.tensor.matmul(db[:, 0:P], ident_b[:, :], causal_b[:, :], start=True, stop=True)
                return last

            def turned(src, f):
                for t in range(4):
                    last = nc.tensor.transpose(db[:, t * P:(t + 1) * P], f(t), ident[:, :])
                return last

            def run(step, done, it):
                kind, *a = step
                if kind == "mx":
                    slot, p, jj, qt = a
                    n = (qt + 1) * P
                    after(pe, max_free, done("mx"))
                    pe.wait_ge(stack_in[slot], done(f"rs{slot}") * (2 * SPLIT * 16))
                    for j in (range(2) if jj is None else (jj,)):
                        base = j * HB if jj is None else 0
                        h = 2 * p + j
                        for k0 in range(0, n, HB):
                            w = min(HB, n - k0)
                            nc.tensor.matmul(mxs[:, base + k0:base + k0 + w],
                                             q_st[0:KS, slot, h, qt * P:(qt + 1) * P],
                                             k_st[0:KS, slot, h, k0:k0 + w], start=True, stop=True)
                        last = nc.tensor.matmul(mxs[:, base + n - P:base + n], ident_b[:, :], causal_b[:, :],
                                                start=False, stop=True, skip_group_check=True)
                    last.then_inc(max_full, 1)
                elif kind == "qk":
                    slot, ch, kt = a
                    q0 = max(kt * P, ch * HB)
                    n = (ch + 1) * HB - q0
                    if (ch, kt) == UNITS[0]:
                        pe.wait_ge(m_row_in, done("nm") * (HG * 16))
                    for p in range(2):
                        after(pe, exp_done, 2 * done("qk") - 1 + p)
                        for jj in range(2):
                            h = 2 * p + jj
                            last = nc.tensor.matmul(st[:, p, jj, 0:n],
                                                    k_st[0:KS + 2, slot, h, kt * P:(kt + 1) * P],
                                                    q_st[0:KS + 2, slot, h, q0:q0 + n], start=True, stop=True)
                        last.then_inc(scores_ready, 1)
                elif kind == "pv":
                    slot, ch, kt = a
                    q0 = max(kt * P, ch * HB)
                    n = (ch + 1) * HB - q0
                    par = UNITS.index((ch, kt)) % 2
                    if kt == 0:
                        after(pe, ov_free, done("ov"))
                        pe.wait_ge(vg_ready, done("vg"))
                    pe.wait_ge(exp_done, 2 * done("pv") + 2)
                    if kt // 4 == ch:
                        pe.wait_ge(masked, done("pv diagonal") + 1)
                    for j in range(HG):
                        last = nc.tensor.matmul(ov[32 * j:32 * j + 32, HB - n:HB], v_g[:, slot, kt, j, :],
                                                probs[:, par, j // 2, j % 2, 0:n],
                                                start=(kt == 0), stop=(kt == 4 * ch + 3))
                    last.then_inc(pv_done, 1)
                elif kind in DENSE:
                    after(pe, dense_free, done("dense"))
                    if kind == "su":
                        last = setup(a[0])
                    elif kind == "t1":
                        k, half = divmod(a[0], 2)
                        pe.wait_ge(norm1_ready, done("ln1"))
                        last = turned(xin, lambda t: xin[:, 4 * half + t, k * P:(k + 1) * P])
                    elif kind == "t2":
                        k, half = divmod(a[0], 2)
                        pe.wait_ge(norm2_ready, done("ln2"))
                        last = turned(x2n, lambda t: x2n[:, 4 * half + t, k * P:(k + 1) * P])
                    elif kind == "ct":
                        k, half = divmod(a[0], 2)
                        last = turned(ctx_n, lambda t: ctx_n[:, 4 * half + t, k * P:(k + 1) * P])
                    elif kind == "ce":
                        pe.wait_ge(ov_free, done("ov"))
                        last = turned(o_sb, lambda t: o_sb[:, a[1], t * P:(t + 1) * P])
                    elif kind == "rb":
                        pe.wait_ge(route_ready, done("ro"))
                        last = turned(ratio_w, lambda t: ratio_w[:, 4 * a[0] + t, :])
                    elif kind == "mt":
                        pe.wait_ge(route_ready, done("ro"))
                        for t in range(T):
                            last = nc.tensor.transpose(db_b[0:KS, t * P:(t + 1) * P],
                                                       low_w[:, a[0], t].rearrange("p s n -> p (s n)"), ident_b[:, :])
                    elif kind == "nm":
                        pe.wait_ge(negm_split, done("ms"))
                        for t in range(T):
                            last = nc.tensor.transpose(db_b[0:2 * HG, t * P:(t + 1) * P],
                                                       m_w[:, t].rearrange("p j s -> p (j s)"), ident_b[:, :])
                    elif kind == "pj":
                        which, ot, half = a
                        for k in range(KC):
                            last = nc.tensor.matmul(db[:, :], w_t[:, WNAMES.index(which), k, ot * P:(ot + 1) * P],
                                                    h_t[:, k, half * HB:(half + 1) * HB],
                                                    start=(k == 0), stop=(k == KC - 1))
                    elif kind in ("vp", "op"):
                        src, m = (h_t, 2) if kind == "vp" else (c_t, 3)
                        for n in range(2):
                            t = 2 * a[0] + n
                            for k in range(KC):
                                last = nc.tensor.matmul(db[:, n * D:(n + 1) * D], src[:, k, t * P:(t + 1) * P],
                                                        w_t[:, m, k, :], start=(k == 0), stop=(k == KC - 1))
                    elif kind == "rt":
                        for k in range(KC):
                            for j in range(4):
                                last = nc.tensor.matmul(db[32 * j:32 * j + 32, 0:D], rout_t[:, k, :],
                                                        c_t[:, k, j * D:(j + 1) * D],
                                                        start=(k == 0), stop=(k == KC - 1))
                    elif kind == "rx":
                        for s in range(2):
                            last = nc.tensor.transpose(db[:, s * P:(s + 1) * P], rout_sb[:, s * P:(s + 1) * P],
                                                       ident[:, :])
                    elif kind == "fa":
                        half, ft = a
                        for k in range(KC):
                            nc.tensor.matmul(db[:, :], wi_t[:, k, ft * P:(ft + 1) * P],
                                             c_t[:, k, half * HB:(half + 1) * HB], start=(k == 0), stop=False)
                        last = nc.tensor.matmul(db[:, :], b_stack[0:KS, ft * P:(ft + 1) * P],
                                                low_st[0:KS, 0, half * HB:(half + 1) * HB], start=False, stop=True)
                    elif kind == "fb":
                        half, ft = a
                        last = nc.tensor.matmul(db[:, :], b_stack[0:KS, ft * P:(ft + 1) * P],
                                                low_st[0:KS, 1, half * HB:(half + 1) * HB], start=False, stop=True,
                                                skip_group_check=True)
                    elif kind == "w":
                        half, t = a
                        pe.wait_ge(hid_ready, done("fb"))
                        for ft in range(FT):
                            last = nc.tensor.matmul(db[:, 0:D], hid[:, ft, t * P:(t + 1) * P], wo_t[:, ft, :],
                                                    start=(ft == 0), stop=(ft == FT - 1))
                    last.then_inc(dense_full, 1)

            walk(pe, NB, run)

        @block.scalar
        def _(act):
            def setup(i):
                if i == 0:
                    act.wait_ge(cond_in, 16)
                    nc.scalar.activation(c_sig[0:NB, :], c_raw[0:NB, :], ACT.Exp, scale=-1.0).then_inc(cond_exp, 1)
                act.wait_ge(dense_full, i + 1)
                if i == 0:
                    return nc.scalar.copy(cond_t, db[:, 0:KC * NB].rearrange("p (k b) -> p k b", k=KC))
                if i == 1:
                    return nc.scalar.copy(mod_t[:, :, :].rearrange("p b n -> p n b"),
                                          db[:, 0:8 * NB].rearrange("p (n b) -> p n b", b=NB))
                if i == 2:
                    return nc.scalar.copy(gate_raw[0:NB, :], db[0:NB, :])
                if i <= 4:
                    return nc.scalar.mul(bt_pad[0:R, 2 * (i - 3):2 * (i - 3) + 2, :],
                                         db[0:R, :].rearrange("p (m d) -> p m d", m=2), LORA_SCALE)
                if i <= 8:
                    return nc.scalar.copy(w_t[:, i - 5, :, :], db[:, :].rearrange("p (k d) -> p k d", k=KC))
                if i <= 12:
                    k, half = divmod(i - 9, 2)
                    return nc.scalar.copy(wi_t[:, k, half * HB:(half + 1) * HB], db[:, :])
                if i <= 16:
                    return nc.scalar.copy(wo_t[:, 2 * (i - 13):2 * (i - 13) + 2, :],
                                          db[:, :].rearrange("p (k d) -> p k d", k=2))
                if i == 17:
                    return nc.scalar.copy(rout_t[:, :, :], db[:, 0:KC * 32].rearrange("p (k n) -> p k n", k=KC))
                if i == 18:
                    return nc.scalar.copy(b_stack[0:KS, :], db_b[0:KS, :])
                return nc.scalar.copy(rest[:, 0, 0:P], db[:, 0:P])

            def run(step, done, it):
                kind, *a = step
                if kind == "qk":
                    slot, ch, kt = a
                    n = (ch + 1) * HB - max(kt * P, ch * HB)
                    par = UNITS.index((ch, kt)) % 2
                    after(act, pv_done, done("pv"))
                    for p in range(2):
                        act.wait_ge(scores_ready, 2 * done("qk") + p + 1)
                        nc.scalar.activation(probs[:, par, p, :, 0:n], st[:, p, :, 0:n], ACT.Exp,
                                             scale=SCORE_SCALE).then_inc(exp_done, 1)
                    return
                if kind == "ov":
                    act.wait_ge(pv_done, done("pv"))
                    nc.scalar.copy(o_sb[:, a[0], :], ov[:, :]).then_inc(ov_free, 1)
                    return
                if kind == "ro":
                    act.wait_ge(route_diff, done("ro") + 1)
                    nc.scalar.activation(rv[:, 1], rv[:, 0], ACT.Exp).then_inc(route_exp, 1)
                    return
                if kind == "su":
                    setup(a[0]).then_inc(dense_free, 1)
                    if a[0] == 5:
                        act.wait_ge(setup_chain, 17)
                        act.dma_start(gates_d, gate_raw[0:NB, :]).then_inc(gates_out, 16)
                    return
                if kind not in ("t1", "t2", "pj", "vp", "ct", "rt", "mt", "rb", "fa", "nm"):
                    return
                act.wait_ge(dense_full, done("dense") + 1)
                if kind in ("t1", "t2"):
                    k, half = divmod(a[0], 2)
                    dst, mod = (h_t, mod1) if kind == "t1" else (c_t, mod2)
                    nc.scalar.activation(dst[:, k, half * HB:(half + 1) * HB], db[:, :], ACT.Identity,
                                         scale=mod[:, 2 + k:3 + k], bias=mod[:, k:k + 1]).then_inc(dense_free, 1)
                elif kind == "pj":
                    which, ot, half = a
                    dst = (q_part if which == "q" else k_part)[:, ot, :, half * HB:(half + 1) * HB]
                    if isinstance(it, int) and it < 0:
                        act.wait_ge(gates_out, 16)
                    after(act, parts_out[ot], done(f"ps{ot}") * (2 * 16))
                    nc.scalar.copy(dst[:, 0, :], db[:, :]).then_inc(part1_ready, 1)
                elif kind == "vp":
                    after(act, vg_ready, done("vg"))
                    nc.scalar.copy(v_st[:, 2 * a[0]:2 * a[0] + 2, :],
                                   db[:, :].rearrange("p (t d) -> p t d", t=2)).then_inc(dense_free, 1)
                elif kind == "ct":
                    k, half = divmod(a[0], 2)
                    nc.scalar.copy(c_t[:, k, half * HB:(half + 1) * HB], db[:, :]).then_inc(dense_free, 1)
                elif kind == "rt":
                    nc.scalar.copy(rout_sb[:, :], db[:, 0:D]).then_inc(dense_free, 1)
                elif kind == "mt":
                    nc.scalar.copy(low_st[0:KS, a[0], :], db_b[0:KS, :]).then_inc(dense_free, 1)
                elif kind == "rb":
                    nc.scalar.copy(ratio_b[:, a[0], :], db[:, :]).then_inc(dense_free, 1)
                elif kind == "fa":
                    half, ft = a
                    nc.scalar.activation(hid[:, ft, :], db[:, :], ACT.Relu).then_inc(dense_free, 1)
                elif kind == "nm":
                    nc.scalar.copy(m_row[:, :], db_b[0:2 * HG, :]).then_inc(dense_free, 1)
                    act.wait_ge(dense_free, done("dense") + 1)
                    for j in range(HG):
                        act.dma_start(q_st[KS:KS + 2, a[0], j, :], m_row[2 * j:2 * j + 2, :]).then_inc(m_row_in, 16)

            walk(act, NB, run)

        @block.vector
        def _(dve):
            links = {"setup": 0}

            def setup_link(ins):
                links["setup"] += 1
                ins.then_inc(setup_chain, 1)
                dve.wait_ge(setup_chain, links["setup"])

            def setup_before():
                nc.vector.memset(k_st[KS:KS + 2, :, :, :], 1.0).then_inc(consts_ready, 1)
                dve.wait_ge(cond_exp, 1)
                setup_link(nc.vector.tensor_scalar_add(c_sig[0:NB, :], c_sig[0:NB, :], 1.0))
                setup_link(nc.vector.reciprocal(c_sig[0:NB, :], c_sig[0:NB, :]))
                setup_link(nc.vector.tensor_tensor(c_sil[0:NB, :], c_sig[0:NB, :], c_raw[0:NB, :], ALU.mult))
                dve.wait_ge(expert_in, 16 * (1 + E))
                setup_link(nc.vector.tensor_copy(eb_w[:, :, 0, :], eb_raw))
                setup_link(nc.vector.tensor_tensor(eb_rest, eb_raw, eb_w[:, :, 0, :], ALU.subtract))
                setup_link(nc.vector.tensor_copy(eb_w[:, :, 1, :], eb_rest))
                setup_link(nc.vector.tensor_tensor(eb_w[:, :, 4, :], eb_rest, eb_w[:, :, 1, :], ALU.subtract))
                setup_link(nc.vector.tensor_copy(eb_w[:, :, 2, :], eb_w[:, :, 0, :]))
                setup_link(nc.vector.tensor_copy(eb_w[:, :, 3, :], eb_w[:, :, 1, :]))
                setup_link(nc.vector.tensor_copy(eb_w[:, :, 5, :], eb_w[:, :, 0, :]))
                setup_link(nc.vector.memset(negm[:, :, :], 0.0))

            def setup_gates():
                dve.wait_ge(dense_free, 3)
                setup_link(nc.vector.tensor_scalar_add(mod_t[:, :, 2:4], mod_t[:, :, 2:4], 1.0))
                setup_link(nc.vector.tensor_scalar_add(mod_t[:, :, 6:8], mod_t[:, :, 6:8], 1.0))
                setup_link(nc.vector.tensor_scalar(gate_sgn[0:NB, :], gate_raw[0:NB, :], 0.0, 2.0,
                                                   ALU.is_ge, ALU.mult))
                setup_link(nc.vector.scalar_tensor_tensor(
                    out=gate_abs[0:NB, :], in0=gate_raw[0:NB, :], scalar=-1.0, in1=gate_raw[0:NB, :],
                    op0=ALU.mult, op1=ALU.max))
                setup_link(nc.vector.tensor_scalar(gate_abs[0:NB, :], gate_abs[0:NB, :], GATE_MIN, None, ALU.max))
                setup_link(nc.vector.scalar_tensor_tensor(
                    out=gate_raw[0:NB, :], in0=gate_sgn[0:NB, :], scalar=-1.0, in1=gate_abs[0:NB, :],
                    op0=ALU.add, op1=ALU.mult))

            def layer_norm(src, dst, n, ready):
                k = [0]

                def link(ins):
                    k[0] += 1
                    ins.then_inc(norm_chain, 1)
                    dve.wait_ge(norm_chain, n * NORM_LINKS + k[0])

                for t in range(T):
                    last = nc.vector.bn_stats(stats[:, t, :], src[:, t, :])
                    k[0] += 1
                    last.then_inc(norm_chain, 1)
                dve.wait_ge(norm_chain, n * NORM_LINKS + k[0])
                nc.vector.memset(fence[:, 3:4], 0.0)
                for t in range(T):
                    last = nc.vector.bn_aggr(mv[:, t, :], stats[:, t, :])
                    k[0] += 1
                    last.then_inc(norm_chain, 1)
                dve.wait_ge(norm_chain, n * NORM_LINKS + k[0])
                var, y, b, sq = (nt[:, i, :] for i in range(4))
                link(nc.vector.tensor_scalar_add(var, mv[:, :, 1], LN_EPS))
                link(nc.vector.tensor_scalar(b.bitcast(I32), var.bitcast(I32), 1, None, ALU.arith_shift_right))
                link(nc.vector.tensor_scalar(y.bitcast(I32), b.bitcast(I32), -1.0, RSQRT_SEED, ALU.mult, ALU.add))
                for _ in range(3):
                    link(nc.vector.tensor_tensor(sq, y, y, ALU.mult))
                    link(nc.vector.scalar_tensor_tensor(out=b, in0=sq, scalar=-0.5, in1=var, op0=ALU.mult,
                                                        op1=ALU.mult))
                    link(nc.vector.scalar_tensor_tensor(out=y, in0=b, scalar=1.5, in1=y, op0=ALU.add,
                                                        op1=ALU.mult))
                assert k[0] == NORM_LINKS
                for t in range(T):
                    last = nc.vector.tensor_scalar(dst[:, t, :], src[:, t, :], mv[:, t, 0:1], y[:, t:t + 1],
                                                   ALU.subtract, ALU.mult)
                last.then_inc(ready, 1)

            def route(n, it):
                k = [0]

                def link(ins):
                    k[0] += 1
                    ins.then_inc(route_chain, 1)
                    dve.wait_ge(route_chain, n * ROUTE_LINKS + k[0])

                d, ex, v, sel1, d2, v2, sel2, wt = (rv[:, i] for i in range(8))
                top, s1, m2, s2, total, w1, r = (rs_[:, i] for i in range(7))

                def wide(s):
                    return s.unsqueeze(2).broadcast_to([P, T, E])

                link(nc.vector.tensor_tensor(wt, lg[:, :, 0:E], bg_b[:, :].unsqueeze(1).broadcast_to([P, T, E]),
                                             ALU.add))
                link(nc.vector.tensor_reduce(top, wt, axis=AX.X, op=ALU.max))
                nc.vector.tensor_tensor(d, wt, wide(top), ALU.subtract).then_inc(route_diff, 1)
                dve.wait_ge(route_diff, n + 1)
                link(nc.vector.scalar_tensor_tensor(out=v, in0=d, scalar=0.0, in1=prio[:, :, :],
                                                    op0=ALU.is_equal, op1=ALU.mult))
                link(nc.vector.tensor_reduce(s1, v, axis=AX.X, op=ALU.max))
                link(nc.vector.tensor_tensor(sel1, v, wide(s1), ALU.is_equal))
                link(nc.vector.scalar_tensor_tensor(out=d2, in0=sel1, scalar=BIG, in1=d, op0=ALU.mult, op1=ALU.add))
                link(nc.vector.tensor_reduce(m2, d2, axis=AX.X, op=ALU.max))
                link(nc.vector.tensor_tensor(d2, d2, wide(m2), ALU.subtract))
                link(nc.vector.scalar_tensor_tensor(out=v2, in0=d2, scalar=0.0, in1=prio[:, :, :],
                                                    op0=ALU.is_equal, op1=ALU.mult))
                link(nc.vector.tensor_reduce(s2, v2, axis=AX.X, op=ALU.max))
                link(nc.vector.tensor_tensor(sel2, v2, wide(s2), ALU.is_equal))
                dve.wait_ge(route_exp, n + 1)
                link(nc.vector.tensor_reduce(total, ex, axis=AX.X, op=ALU.add))
                link(nc.vector.reciprocal(w1, total))
                link(nc.vector.tensor_tensor(wt, ex, sel2, ALU.mult))
                link(nc.vector.tensor_reduce(r, wt, axis=AX.X, op=ALU.add))
                link(nc.vector.tensor_copy(ratio_w[:, :, :], r.unsqueeze(2).broadcast_to([P, T, P])))
                link(nc.vector.tensor_tensor(d2, sel2, sel1, ALU.subtract))
                low = lg[:, :, E:E + DH].rearrange("p t (e r) -> p t e r", e=E)
                for i, mask in enumerate((sel1, d2)):
                    last = nc.vector.tensor_tensor(
                        lowf[:, i].rearrange("p t (e r) -> p t e r", e=E), low,
                        mask.unsqueeze(3).broadcast_to([P, T, E, RK]), ALU.mult)
                    if i == 0:
                        k[0] += 1
                        last.then_inc(route_chain, 1)
                link(last)
                full = lowf[:, :, :, :].rearrange("p v t n -> p (v t) n")
                left = lowr[:, :, :, :].rearrange("p v t n -> p (v t) n")
                stack = low_w[:, :, :, :, :].rearrange("p v t s n -> p (v t) s n")
                nvt = 2 * T
                link(nc.vector.tensor_copy(stack[:, :, 0:2, :], full.unsqueeze(2).broadcast_to([P, nvt, 2, DH])))
                nc.vector.tensor_copy(stack[:, :, 4, :], full).then_inc(route_chain, 1)
                k[0] += 1
                link(nc.vector.tensor_tensor(left, full, stack[:, :, 0, :], ALU.subtract))
                link(nc.vector.tensor_copy(stack[:, :, 2:4, :], left.unsqueeze(2).broadcast_to([P, nvt, 2, DH])))
                assert k[0] == ROUTE_LINKS, k[0]
                nc.vector.tensor_tensor(stack[:, :, 5, :], left, stack[:, :, 2, :],
                                        ALU.subtract).then_inc(route_ready, 1)

            def run(step, done, it):
                kind, *a = step
                if kind == "su":
                    if a[0] == 0:
                        setup_before()
                    elif a[0] == 3:
                        setup_gates()
                        dve.wait_ge(consts_ready, 9)
                elif kind == "ln1":
                    dve.wait_ge(xin_in, 16 * (done("ln1") + 1))
                    nc.vector.tensor_copy(mod1[:, :], mod_t[:, it + 1, 0:4] if isinstance(it, int)
                                          else mod_t[:, bass.ds(it + 1, 1), 0:4].rearrange("p b n -> p (b n)"))
                    layer_norm(xin, xin, done("ln1") + done("ln2"), norm1_ready)
                elif kind == "ln2":
                    dve.wait_ge(x1_ready, done("op"))
                    nc.vector.tensor_copy(mod2[:, :], mod_t[:, it - 1, 4:8] if isinstance(it, int)
                                          else mod_t[:, bass.ds(it - 1, 1), 4:8].rearrange("p b n -> p (b n)"))
                    layer_norm(x1, x2n, done("ln1") + done("ln2"), norm2_ready)
                elif kind == "ro":
                    dve.wait_ge(dense_free, done("dense"))
                    route(done("ro"), it)
                elif kind == "mx":
                    slot, p, jj, qt = a
                    n = (qt + 1) * P
                    dve.wait_ge(max_full, done("mx") + 1)
                    if jj is None:
                        src = mxs[:, :].rearrange("p (j k) -> p j k", j=2)[:, :, 0:n]
                        dst = negm[:, qt, 2 * p:2 * p + 2]
                    else:
                        src = mxs[:, 0:n]
                        dst = negm[:, qt, 2 * p + jj:2 * p + jj + 1]
                    nc.vector.tensor_reduce(dst, src, axis=AX.X, op=ALU.max, negate=True).then_inc(max_free, 1)
                elif kind == "vg":
                    g = a[0]
                    after(dve, dense_free, done("dense"))
                    after(dve, pv_done, done("pv"))
                    nc.vector.tensor_copy(
                        v_g[:, g % 2, :, :, 0:DH],
                        v_st[:, :, HG * DH * g:HG * DH * (g + 1)].rearrange("p t (j d) -> p t j d", j=HG)
                    ).then_inc(vg_ready, 1)
                elif kind == "ms":
                    dve.wait_ge(max_free, done("mx"))
                    nc.vector.tensor_copy(m_w[:, :, :, 0], negm[:, :, :]).then_inc(negm_hi, 1)
                    dve.wait_ge(negm_hi, done("ms") + 1)
                    nc.vector.tensor_tensor(m_w[:, :, :, 1], negm[:, :, :], m_w[:, :, :, 0],
                                            ALU.subtract).then_inc(negm_split, 1)
                elif kind == "pj":
                    which, ot, half = a
                    dst = (q_part if which == "q" else k_part)[:, ot, :, half * HB:(half + 1) * HB]
                    par = 0 if which == "q" else 1
                    dve.wait_ge(part1_ready, done("pj") + 1)
                    after(dve, part3_ready, done("pj") - 1)
                    nc.vector.tensor_tensor(rest[:, par, :], db[:, :], dst[:, 0, :],
                                            ALU.subtract).then_inc(dense_free, 1)
                    dve.wait_ge(dense_free, done("dense") + 1)
                    nc.vector.tensor_copy(dst[:, 1, :], rest[:, par, :]).then_inc(part2_ready, 1)
                elif kind == "ce":
                    g, ch = a
                    dve.wait_ge(dense_full, done("dense") + 1)
                    o = db[:, :].rearrange("p (q j e) -> p q j e", q=4, j=HG)
                    nc.vector.reciprocal(rsum[:, :, :], o[:, :, :, DH]).then_inc(rsum_ready, 1)
                    dve.wait_ge(rsum_ready, done("ce") + 1)
                    nc.vector.tensor_tensor(
                        ctx_n[:, 4 * ch:4 * ch + 4, HG * DH * g:HG * DH * (g + 1)].rearrange(
                            "p q (j d) -> p q j d", j=HG),
                        o[:, :, :, 0:DH], rsum[:, :, :].unsqueeze(3).broadcast_to([P, 4, HG, DH]),
                        ALU.mult).then_inc(dense_free, 1)
                elif kind == "op":
                    i = a[0]
                    if i == 0:
                        dve.wait_ge(gates_in, 16 * done("xl"))
                    dve.wait_ge(dense_full, done("dense") + 1)
                    if i >= 2:
                        dve.wait_ge(x1_ready, done("op") - 1)
                    nc.vector.tensor_tensor(
                        second[:, i % 2, :].rearrange("p (t d) -> p t d", t=2),
                        db[:, :].rearrange("p (t d) -> p t d", t=2),
                        gates_b[:, 0:D].unsqueeze(1).broadcast_to([P, 2, D]), ALU.mult).then_inc(dense_free, 1)
                elif kind == "rx":
                    dve.wait_ge(dense_full, done("dense") + 1)
                    for s in range(2):
                        last = nc.vector.tensor_copy(
                            lg[:, :, :].rearrange("p (j s) n -> p s j n", s=2)[:, s],
                            db[:, s * P:(s + 1) * P].rearrange("p (j n) -> p j n", j=4)[:, :, 0:E + DH])
                    last.then_inc(dense_free, 1)
                elif kind == "fb":
                    half, ft = a
                    dve.wait_ge(dense_full, done("dense") + 1)
                    if (half, ft) >= (0, 2):
                        dve.wait_ge(hid_ready, done("fb") - 1)
                    nc.vector.scalar_tensor_tensor(out=second[:, ft % 2, :], in0=db[:, :], scalar=0.0,
                                                   in1=ratio_b[:, half, :], op0=ALU.max,
                                                   op1=ALU.mult).then_inc(dense_free, 1)
                elif kind == "w":
                    half, t = a
                    dve.wait_ge(dense_full, done("dense") + 1)
                    after(dve, out_done[t % 2], 16 * done(f"w{t % 2}"))
                    nc.vector.scalar_tensor_tensor(out=ob[:, t % 2, :], in0=db[:, 0:D],
                                                   scalar=rs_[:, 5, 4 * half + t:4 * half + t + 1],
                                                   in1=gates_b[:, D:2 * D], op0=ALU.mult,
                                                   op1=ALU.mult).then_inc(dense_free, 1)

            walk(dve, NB, run)


_INS = ["L0_attn_x", "L0_attn_wq", "L0_attn_aq", "L0_attn_bq", "L0_attn_wk", "L0_attn_ak", "L0_attn_bk",
        "L0_attn_wv", "L0_attn_av", "L0_attn_bv", "L0_attn_wo", "L0_attn_ao", "L0_attn_bo", "L0_ffn_Wg",
        "L0_ffn_bg", "L0_ffn_Wi", "L0_ffn_Wo", "L0_ffn_A", "L0_ffn_B", "L0_c", "L0_wmod"]


def kernel(**inputs):
    import numpy as np
    import concourse.bacc as bacc
    from concourse.bass_utils import run_bass_kernel_spmd

    nc = bacc.Bacc("TRN2", target_bir_lowering=False, num_devices=1)
    arrays, args = {}, []
    for name in _INS:
        a = np.ascontiguousarray(inputs[name])
        arrays[f"in_{name}"] = a
        args.append(nc.dram_tensor(f"in_{name}", a.shape, mybir.dt.from_np(a.dtype), kind="ExternalInput").ap())
    x = inputs["L0_attn_x"]
    args.append(nc.dram_tensor("out_x", x.shape, F32, kind="ExternalOutput").ap())
    adaln_block(nc, *args)
    r = run_bass_kernel_spmd(nc, [arrays], core_ids=[0])
    return r.results[0]["out_x"]
```

```python
from contextlib import ExitStack

import concourse.bass as bass
from concourse import mybir

F32 = mybir.dt.float32
BF16 = mybir.dt.bfloat16
I32 = mybir.dt.int32
ALU = mybir.AluOpType
ACT = mybir.ActivationFunctionType
AX = mybir.AxisListType

P = 128
DH = 16
HG = 4
SPLIT = 6
Q_PARTS = (0, 0, 1, 1, 0, 2)
K_PARTS = (0, 1, 0, 1, 2, 0)
KS = SPLIT * DH
BIG = -3.0e38
LN_EPS = 1e-5
RSQRT_SEED = float(0x5F3759DF)
GATE_MIN = 0.25

DENSE = frozenset("su t1 pj vp ct op t2 rt rx mt rb fa w ce nm".split())


def attention_units():
    return [(c, kt) for c in range(2) for kt in range(4 * (c + 1))]


UNITS = attention_units()
NU = len(UNITS)
GROUPS = 4
V_NEEDED = 44
V_FREE = 33


def max_steps():
    steps = []
    for qt in range(7, -1, -1):
        if qt >= 4:
            steps += [(h, 1, qt, 0) for h in range(HG)]
        heads = {0: 4, 1: 2}.get(qt % 4, 1)
        steps += [(h, heads, qt, qt // 4) for h in range(0, HG, heads)]
    return steps


def max_keys(qt, chunk):
    return min((qt + 1) * P - chunk * 512, 512)


def pe_cost(step):
    if step[0] == "mx":
        _, _, _, heads, qt, chunk = step
        return (max_keys(qt, chunk) + P * (qt // 4 == chunk)) * heads / 2.4
    return {"ct": 300, "op": 1750, "t1": 300, "t2": 300, "rt": 1000, "rx": 200, "mt": 500, "rb": 300,
            "pj": 1750, "vp": 1750, "fa": 1950, "fb": 250, "w": 3500, "ce": 450, "nm": 850}.get(step[0], 0)


def body_plan(pre, post, lead):
    queue = []

    def put(unit, *steps):
        queue.extend((unit, (s,)) for s in steps)

    early = [("pj", w, ot, half) for ot in range(2) for half in range(2) for w in "qk"]
    early.insert(4, ("ps", 0))
    late = [("vp", i) for i in range(4)]
    if post:
        put(0, ("ce", GROUPS - 1, 1), *[("ct", i) for i in range(4)], *[("op", i) for i in range(4)])
    if pre:
        put(0, ("ln1",))
        put(3, *[("t1", i) for i in range(4)])
        put(4, *early[:5])
    if post:
        put(10, ("ln2",))
    if pre:
        put(11, early[5])
    if post:
        put(12, *[("t2", i) for i in range(4)], ("rt",), ("rx",), ("ro",))
    if pre:
        put(13, early[6])
    if post:
        put(13, *[("mt", v) for v in range(2)], *[("rb", half) for half in range(2)])
        for half in range(2):
            for quad in hidden_quads(half):
                queue.append((8, quad))
                if half and pre:
                    put(V_FREE, late[quad[0][2] // 2])
            if not half and pre:
                put(8, *early[-2:])
            put(8, *[("w", half, t) for t in range(4)])
    elif pre:
        put(8, *early[-2:])
        put(V_FREE, *late)
    unit_cost = [8 * 512 / 2.4 if kt < 4 * c else 8 * (512 - 128 * (kt % 4)) / 2.4 for c, kt in UNITS]
    row_maxima = [[0, 0, 4, 4, 5, 5, 5, 5, 5, 5, 0, 0]] * GROUPS
    row_maxima[0] = [0, 0, 0, 5, 5, 5, 5, 6, 6, 6, 0, 0]
    parts_left = pre
    fixed = 8 * pe_cost(("ce",)) + 4 * pe_cost(("nm",))
    total = GROUPS * (sum(unit_cost) + sum(pe_cost(("mx", 0, *s)) for s in max_steps())) + fixed
    total += sum(pe_cost(s) for _, q in queue for s in q)
    spent = 0.0
    plan = []
    if pre:
        plan.append(("xin",))
    if post:
        plan.append(("xl",))
    for u in range(GROUPS * NU):
        g, k = divmod(u, NU)
        c, kt = UNITS[k]
        more = lead or g < GROUPS - 1
        pinned = []
        if k == NU - 2 and more:
            pinned.append(("nm", (g + 1) % 2))
        if k in (4, 0) and u > 0:
            pinned.append(("ce", g, 0) if k == 4 else ("ce", g - 1, 1))
        fillers = []
        first = sum(row_maxima[g][:k])
        mx = [("mx", (g + 1) % 2, *s) for s in max_steps()[first:first + row_maxima[g][k]]] if more else []
        spent += unit_cost[k] + sum(map(pe_cost, mx + pinned))
        goal = total * (u + 1) / (GROUPS * NU)
        while queue and queue[0][0] <= u and (spent + sum(map(pe_cost, queue[0][1])) / 2 <= goal
                                              or u == GROUPS * NU - 1 or u == V_NEEDED - 1 and late[-1] in [
                                                  s for _, q in queue for s in q]):
            fillers.append(queue[0][1])
            spent += sum(map(pe_cost, queue.pop(0)[1]))
        following = []
        if u + 1 < GROUPS * NU or lead:
            following = [("qk", (u + 1) // NU % 2, *UNITS[(u + 1) % NU], j) for j in range(HG)]
        if k == NU - 1 and (pre or g < 2):
            plan.append(("rs", g % 2, (g + 2) % GROUPS))
        half = (len(fillers) + 1) // 2
        half = 0 if k == NU - 2 else half
        together = [s for q in fillers[:half] + [pinned] + fillers[half:] for s in q]
        lo = 0.75 if k == NU - 1 else 0.0
        turns = [(lo + (1 - lo) * (i + 0.5) / HG, 0, s) for i, s in enumerate(following)]
        turns += [((i + 0.5) / len(part), n, s) for n, part in ((1, mx), (2, together)) for i, s in enumerate(part)]
        for _, n, s in sorted(turns, key=lambda turn: turn[:2]):
            plan.append(s)
            if n == 1 and s is mx[-1] and k == 9:
                plan.append(("ms",))
        if parts_left and u >= 2 * NU and not any(s in early for _, q in queue for s in q):
            plan.append(("ps", 1))
            parts_left = False
        plan.append(("pv", g % 2, c, kt))
        if kt == 4 * c + 3:
            plan.append(("ov", c))
        if k == 8 and more:
            plan.append(("vg", (g + 1) % GROUPS))
    assert not queue
    at = {s: i for i, s in enumerate(plan)}
    if pre:
        assert at["vp", 3] < at["vg", 0] and at["ps", 0] < at["rs", 0, 0] and at["ps", 1] < at["rs", 1, 1]
    return plan


def hidden_quads(half):
    return [(("fa", half, ft), ("fa", half, ft + 1), ("fb", half, ft), ("fb", half, ft + 1))
            for ft in range(0, 8, 2)]


def prologue_plan():
    plan = [("su", i) for i in range(N_SETUP)]
    plan += [("ln1",)] + [("t1", i) for i in range(4)]
    for ot in range(2):
        plan += [("pj", w, ot, half) for half in range(2) for w in "qk"] + [("ps", ot)]
    plan += [("vp", i) for i in range(4)]
    plan += [("rs", 0, 0), ("rs", 1, 1), ("vg", 0)]
    plan += [("mx", 0, *s) for s in max_steps()] + [("ms",), ("nm", 0)] + [("qk", 0, *UNITS[0], j) for j in range(HG)]
    return plan


def epilogue_plan():
    plan = [("xl",), ("ce", GROUPS - 1, 1)] + [("ct", i) for i in range(4)] + [("op", i) for i in range(4)]
    plan += [("ln2",)] + [("t2", i) for i in range(4)] + [("rt",), ("rx",), ("ro",)]
    plan += [("mt", v) for v in range(2)] + [("rb", half) for half in range(2)]
    for half in range(2):
        for quad in hidden_quads(half):
            plan += quad
        plan += [("w", half, t) for t in range(4)]
    return plan


N_SETUP = 20


def tallied(step, bank):
    names = [step[0]]
    if step[0] in DENSE:
        names.append(f"bank{bank}")
    if step[0] in DENSE and step[0] != "fa" or step[0] == "fb":
        names.append("full")
    if step[0] == "pv" and step[2] == step[3] // 4:
        names.append("pv diagonal")
    if step[0] == "qk" and step[2] == step[3] // 4 and step[4] == HG - 1:
        names.append("qk diagonal")
    if step[0] in ("rs", "ps"):
        names.append(f"{step[0]}{step[1]}")
    if step[0] == "w":
        names.append(f"w{step[2] % 2}")
    return names


def with_banks(plan, first):
    n, steps, hidden = first, [], {}
    for s in plan:
        bank = None
        if s[0] in DENSE:
            bank = n % 2
            n += 1
            if s[0] == "fa":
                hidden[s[1:]] = bank
        elif s[0] == "fb":
            bank = hidden[s[1:]]
        steps.append((s, bank))
    return steps, n % 2


def walk(eng, batches, run):
    counts = {}
    bank_next = [0]

    def phase(plan, it, reg):
        first = bank_next[0]
        steps, bank_next[0] = with_banks(plan, first)
        assert reg is None or bank_next[0] == first
        per = {}
        for s, bank in steps:
            for n in tallied(s, bank):
                per[n] = per.get(n, 0) + 1
        here = {}
        for s, bank in steps:
            def done(name, here=dict(here)):
                fixed = counts.get(name, 0) + here.get(name, 0)
                return fixed if reg is None or not per.get(name) else reg * per[name] + fixed
            run(s, done, it, bank)
            for n in tallied(s, bank):
                here[n] = here.get(n, 0) + 1
        for n, m in per.items():
            counts[n] = counts.get(n, 0) + m * (1 if reg is None else batches - 2)

    phase(prologue_plan(), -1, None)
    phase(body_plan(pre=True, post=False, lead=True), 0, None)
    with eng.Fori(0, batches - 2) as reg:
        phase(body_plan(pre=True, post=True, lead=True), reg + 1, reg)
    phase(body_plan(pre=False, post=True, lead=False), batches - 1, None)
    phase(epilogue_plan(), batches, None)


def after(eng, sem, value):
    if not isinstance(value, int) or value > 0:
        eng.wait_ge(sem, value)


def held(eng, value):
    return value if isinstance(value, int) else eng.to_reg(value)


def adaln_block(nc, x, wq, aq, bq, wk, ak, bk, wv, av, bv, wo, ao, bo, Wg, bg, Wi, Wo, A, Bm, c, wmod, out):
    NB, S, D = x.shape
    R = aq.shape[0]
    F = Wi.shape[0]
    E, RK, _ = A.shape
    T = S // P
    KC = D // P
    FT = F // P
    HB = S // 2
    LORA_SCALE = 1.0 / R
    SCORE_SCALE = float(DH) ** -0.5
    assert (S, D, R, F, E * RK, NB) == (1024, 256, DH, 1024, DH, 8)

    x_t = x.rearrange("b (t p) d -> b p t d", p=P)
    out_t = out.rearrange("b (t p) d -> b t p d", p=P)

    with ExitStack() as ctx:
        def sb(name, shape, dt=F32):
            return ctx.enter_context(nc.sbuf_tensor(name, shape, dt))

        def sem(name):
            return ctx.enter_context(nc.semaphore(name))

        ident = sb("ident", [P, P])
        ident_b = sb("ident_b", [P, P], BF16)
        causal_b = sb("causal_b", [P, P], BF16)
        w_t = sb("w_t", [P, 4, KC, D])
        wi_t = sb("wi_t", [P, KC, F])
        wo_t = sb("wo_t", [P, FT, D])
        rout_t = sb("rout_t", [P, KC, 32])
        b_stack = sb("b_stack", [P, F], BF16)
        bg_b = sb("bg_b", [P, E])
        prio = sb("prio", [P, T, E])
        mod_t = sb("mod_t", [P, NB, 8])
        mod1 = sb("mod1", [P, 4])
        mod2 = sb("mod2", [P, 4])
        gates_b = sb("gates_b", [P, 2 * D])
        xin = sb("xin", [P, T, D])
        x1 = sb("x1", [P, T, D])
        h_t = sb("h_t", [P, KC, S])
        ctx_n = sb("ctx_n", [P, T, D])
        c_t = sb("c_t", [P, KC, S])
        v_st = sb("v_st", [P, T, D])
        v_g = sb("v_g", [P, 2, T, HG, 32])
        q_part = sb("q_part", [P, 2, 3, S], BF16)
        k_part = sb("k_part", [P, 2, 3, S], BF16)
        rest = sb("rest", [P, 2, HB])
        q_st = sb("q_st", [P, 2, HG, S], BF16)
        k_st = sb("k_st", [P, 2, HG, S], BF16)
        probs = sb("probs", [P, 2, HG, HB])
        o_sb = sb("o_sb", [P, 2, HB])
        hid = sb("hid", [P, FT, HB])
        second = sb("second", [P, 2, HB])
        ob = sb("ob", [P, 2, D])
        ratio_b = sb("ratio_b", [P, 2, HB])
        low_st = sb("low_st", [P, 2, S], BF16)
        low_w = sb("low_w", [P, 2, T, SPLIT, DH], BF16)
        rout_sb = sb("rout_sb", [P, D])
        m_row = sb("m_row", [8, S], BF16)
        negm = sb("negm", [P, T, HG])
        negm_left = sb("negm_left", [P, T - 4, HG])
        m_w = sb("m_w", [P, T, HG, 2], BF16)
        rsum = sb("rsum", [P, 4, HG])
        stats = sb("stats", [P, T, 6])
        fence = sb("fence", [P, 4])
        mv = sb("mv", [P, T, 2])
        nt = sb("nt", [P, 4, T])
        lg = sb("lg", [P, T, E + DH])
        rv = sb("rv", [P, 8, T, E])
        rs_ = sb("rs_", [P, 8, T])
        lowf = sb("lowf", [P, 2, T, DH])
        lowr = sb("lowr", [P, 2, T, DH])
        ratio_w = second[:, :, :].rearrange("p a (t n) -> p (a t) n", n=P)
        x2n = hid[:, :, :].rearrange("p a b -> p (a b)")[:, 0:T * D].rearrange("p (t d) -> p t d", t=T)

        hid_f = hid[:, :, :].rearrange("p a b -> p (a b)")
        wi_raw = hid_f[:, 0:FT * D].rearrange("p (t d) -> p t d", t=FT)
        wo_raw = hid_f[:, FT * D:2 * FT * D].rearrange("p (t f) -> p t f", t=KC)
        probs_f = probs[:, :, :, :].rearrange("p a b c -> p (a b c)")
        wmod_sb = probs_f[:, 0:KC * 6 * D].rearrange("p (k n) -> p k n", k=KC)
        a_pad = probs_f[:, KC * 6 * D:KC * 6 * D + 4 * D].rearrange("p (m d) -> p m d", m=4)
        qp_f = q_part[:, :, :, :].rearrange("p a b c -> p (a b c)").bitcast(F32)
        w_raw = qp_f[:, 0:4 * KC * D].rearrange("p (m t d) -> p m t d", m=4, t=KC)
        bt_pad = qp_f[:, 2048:2048 + 4 * D].rearrange("p (m d) -> p m d", m=4)
        kp_f = k_part[:, :, :, :].rearrange("p a b c -> p (a b c)").bitcast(F32)
        b_raw = kp_f[:, 0:128].rearrange("p (m t r) -> p m t r", m=4, t=KC)
        eb_raw = kp_f[:, 128:256].rearrange("p (t n) -> p t n", t=FT)
        eb_rest = kp_f[:, 256:384].rearrange("p (t n) -> p t n", t=FT)
        eb_w = k_part[:, 0, 1, 0:FT * KS].rearrange("p (t s n) -> p t s n", t=FT, s=SPLIT)
        r_raw = kp_f[:, 1024:1280]
        c_raw = kp_f[:, 1280:1536]
        c_sig = kp_f[:, 1536:1792]
        c_sil = kp_f[:, 1792:2048]
        cond_t = kp_f[:, 2048:2048 + KC * NB].rearrange("p (k b) -> p k b", k=KC)
        gate_raw = kp_f[:, 2304:2304 + 2 * D]
        gate_abs = o_sb[:, 0, :]
        gate_sgn = o_sb[:, 1, :]

        st = ctx.enter_context(nc.psum_tensor("st", [P, 3, HB], F32))
        ov = ctx.enter_context(nc.psum_tensor("ov", [P, HB], F32))
        mxs = ctx.enter_context(nc.psum_tensor("mxs", [P, 2, HB], F32))
        dense = ctx.enter_context(nc.psum_tensor("dense", [P, 2, HB], F32))

        def dense_bank(bank):
            db = dense[:, bank or 0, :]
            return db, db.bitcast(BF16)

        def evacuated(eng, done):
            for i in range(2):
                after(eng, dense_free[i], done(f"bank{i}"))

        q_d, k_d = (nc.dram_tensor(f"{w}_parts_scratch", [2, P, 3, S], BF16, kind="Internal").ap() for w in "qk")
        gates_d = nc.dram_tensor("gates_scratch", [NB, 2 * D], F32, kind="Internal").ap()

        weights_in = sem("weights_in")
        cond_in = sem("cond_in")
        wmod_in = sem("wmod_in")
        expert_in = sem("expert_in")
        zeroed = sem("zeroed")
        consts_ready = sem("consts_ready")
        gates_out = sem("gates_out")
        setup_chain = sem("setup_chain")
        cond_exp = sem("cond_exp")
        xin_in = sem("xin_in")
        x1_in = sem("x1_in")
        gates_in = sem("gates_in")
        norm1_ready = sem("norm1_ready")
        norm2_ready = sem("norm2_ready")
        norm_chain = sem("norm_chain")
        dense_full = sem("dense_full")
        dense_free = [sem(f"dense_free{i}") for i in range(2)]
        base_full = sem("base_full")
        relu_done = sem("relu_done")
        part1_ready = sem("part1_ready")
        rest_ready = sem("rest_ready")
        part2_ready = sem("part2_ready")
        part3_ready = sem("part3_ready")
        stack_in = [sem(f"stack_in{s}") for s in range(2)]
        parts_out = [sem(f"parts_out{i}") for i in range(2)]
        max_full = sem("max_full")
        max_free = sem("max_free")
        negm_split = sem("negm_split")
        negm_ready = sem("negm_ready")
        negm_hi = sem("negm_hi")
        m_row_in = sem("m_row_in")
        scores_ready = sem("scores_ready")
        exp_done = sem("exp_done")
        fenced = sem("fenced")
        masked = sem("masked")
        vg_ready = sem("vg_ready")
        pv_done = sem("pv_done")
        ov_free = sem("ov_free")
        rsum_ready = sem("rsum_ready")
        x1_ready = sem("x1_ready")
        route_chain = sem("route_chain")
        route_diff = sem("route_diff")
        route_exp = sem("route_exp")
        route_ready = sem("route_ready")
        hid_ready = sem("hid_ready")
        out_scaled = sem("out_scaled")
        out_ready = sem("out_ready")
        out_done = [sem(f"out_done{i}") for i in range(2)]

        WNAMES = "qkvo"
        W_IN = 16 * 16
        NORM_LINKS = 2 * T + 1 + 2 + 3 * 3
        ROUTE_LINKS = 23

        block = ctx.enter_context(nc.Block())

        @block.sync
        def _(sp):
            sp.wait_ge(zeroed, 2)
            sp.dma_start(c_raw[0:NB, :], c).then_inc(cond_in, 16)
            sp.dma_start(xin[:, :, :], x_t[0]).then_inc(xin_in, 16)
            sp.dma_start(wmod_sb, wmod.rearrange("(k p) n -> p k n", p=P)).then_inc(wmod_in, 16)
            for m, (w, a, b) in enumerate(((wq, aq, bq), (wk, ak, bk), (wv, av, bv), (wo, ao, bo))):
                sp.dma_start(w_raw[:, m], w.rearrange("(t p) d -> p t d", p=P)).then_inc(weights_in, 16)
                sp.dma_start(a_pad[0:R, m], a).then_inc(weights_in, 16)
                sp.dma_start(b_raw[:, m], b.rearrange("(t p) r -> p t r", p=P)).then_inc(weights_in, 16)
            sp.dma_start(r_raw[0:E, :], Wg).then_inc(weights_in, 16)
            sp.dma_start(r_raw[E:E + DH, :], A.rearrange("e r d -> (e r) d")).then_inc(expert_in, 16)
            sp.dma_start(wi_raw, Wi.rearrange("(t p) d -> p t d", p=P)).then_inc(weights_in, 16)
            sp.dma_start(wo_raw, Wo.rearrange("(t p) f -> p t f", p=P)).then_inc(weights_in, 16)
            for e in range(E):
                sp.dma_start(eb_raw[:, :, e * RK:(e + 1) * RK],
                             Bm[e].rearrange("(t p) r -> p t r", p=P)).then_inc(expert_in, 16)
            sp.dma_start(bg_b[:, :], bg.partition_broadcast(P)).then_inc(weights_in, 16)

            def run(step, done, it, bank):
                kind, *a = step
                db, db_b = dense_bank(bank)
                if kind == "xin":
                    after(sp, dense_full, done("full"))
                    sp.dma_start(xin[:, :, :], x_t[it + 1]).then_inc(xin_in, 16)
                elif kind == "xl":
                    sp.wait_ge(out_ready, done("w") + 1)
                    sp.dma_start(x1[:, :, :], x_t[it - 1]).then_inc(x1_in, 16)
                    sp.wait_ge(gates_out, 16)
                    sp.dma_start(gates_b[:, :], gates_d[it - 1].partition_broadcast(P)).then_inc(gates_in, 16)
                elif kind == "ps":
                    ot = a[0]
                    stacked = [held(sp, done(f"rs{s}") * (2 * SPLIT * 16)) for s in range(2)]
                    split = held(sp, done("pj"))
                    sp.wait_ge(part3_ready, split)
                    for s in range(2):
                        after(sp, stack_in[s], stacked[s])
                    for dst, src in ((q_d, q_part), (k_d, k_part)):
                        sp.dma_start(dst[ot], src[:, ot, :, :]).then_inc(parts_out[ot], 16)
                elif kind == "rs":
                    slot, g = a
                    ot, lower = divmod(g, 2)
                    scored, stored = held(sp, done("qk")), held(sp, done(f"ps{ot}") * (2 * 16))
                    after(sp, scores_ready, scored)
                    sp.wait_ge(parts_out[ot], stored)
                    rows = slice(lower * HG * DH, (lower + 1) * HG * DH)
                    for s in range(SPLIT):
                        for dst, src, part in ((q_st, q_d, Q_PARTS[s]), (k_st, k_d, K_PARTS[s])):
                            heads = src[ot, rows, part, :].rearrange("(j d) n -> d j n", j=HG)
                            sp.dma_start(dst[s * DH:(s + 1) * DH, slot, :, :], heads).then_inc(stack_in[slot], 16)
                elif kind == "w":
                    half, t = a
                    sp.wait_ge(out_ready, done("w") + 2)
                    sp.dma_start(out_t[it - 1, 4 * half + t], ob[:, t % 2, :]).then_inc(out_done[t % 2], 16)

            walk(sp, NB, run)
            for s in out_done:
                sp.wait_ge(s, 16 * (NB * T // 2 + 1))

        @block.gpsimd
        def _(pool):
            nc.gpsimd.memset(fence[:, 0:3], 0.0).then_inc(consts_ready, 1)
            nc.gpsimd.memset(a_pad, 0.0).then_inc(zeroed, 1)
            nc.gpsimd.memset(r_raw[0:32, :], 0.0).then_inc(zeroed, 1)
            nc.gpsimd.memset(bt_pad, 0.0).then_inc(zeroed, 1)
            nc.gpsimd.memset(ident[:, :], 0.0).then_inc(zeroed, 1)
            nc.gpsimd.memset(causal_b[:, :], 0.0).then_inc(zeroed, 1)
            pool.wait_ge(zeroed, 5)
            nc.gpsimd.affine_select(out=ident[:, :], in_=ident[:, :], compare_op=ALU.not_equal, fill=1.0,
                                    base=0, pattern=[[-1, P]], channel_multiplier=1).then_inc(zeroed, 1)
            pool.wait_ge(zeroed, 6)
            nc.gpsimd.tensor_copy(ident_b[:, :], ident[:, :]).then_inc(consts_ready, 1)
            nc.gpsimd.affine_select(out=causal_b[:, :], in_=causal_b[:, :], compare_op=ALU.is_ge, fill=BIG,
                                    base=0, pattern=[[-1, P]], channel_multiplier=1).then_inc(consts_ready, 1)
            nc.gpsimd.memset(v_g[:, :, :, :, :], 0.0).then_inc(zeroed, 1)
            pool.wait_ge(zeroed, 7)
            nc.gpsimd.memset(v_g[:, :, :, :, DH:DH + 1], 1.0).then_inc(consts_ready, 1)
            for e in range(E):
                nc.gpsimd.memset(prio[:, :, e:e + 1], float(E - e)).then_inc(consts_ready, 1)

            for i in range(2):
                nc.gpsimd.memset(ob[:, i, :], 0.0).then_inc(out_done[i], 16)
            nc.gpsimd.memset(fence[:, 0:1], 0.0).then_inc(out_ready, 1)

            def run(step, done, it, bank):
                kind, *a = step
                if kind == "qk":
                    slot, ch, kt, j = a
                    if kt // 4 == ch and j == HG - 1:
                        par = UNITS.index((ch, kt)) % 2
                        pool.wait_ge(exp_done, done("qk") + 1)
                        after(pool, fenced, done("qk diagonal"))
                        nc.gpsimd.tensor_tensor(fence[:, 0:1], fence[:, 1:2], fence[:, 2:3],
                                                ALU.mult).then_inc(fenced, 1)
                        tri = probs[:, par, :, 0:P]
                        nc.gpsimd.affine_select(
                            out=tri, in_=tri, compare_op=ALU.is_ge, fill=0.0, base=0,
                            pattern=[[0, HG], [1, P]], channel_multiplier=-1).then_inc(masked, 1)
                elif kind == "pj":
                    which, ot, half = a
                    dst = (q_part if which == "q" else k_part)[:, ot, :, half * HB:(half + 1) * HB]
                    par = 0 if which == "q" else 1
                    pool.wait_ge(part2_ready, done("pj") + 1)
                    nc.gpsimd.tensor_tensor(dst[:, 2, :], rest[:, par, :], dst[:, 1, :],
                                            ALU.subtract).then_inc(part3_ready, 1)
                elif kind == "op":
                    i = a[0]
                    if i == 0:
                        pool.wait_ge(x1_in, 16 * (done("xl")))
                    pool.wait_ge(dense_free[bank], done(f"bank{bank}") + 1)
                    nc.gpsimd.tensor_tensor(
                        x1[:, 2 * i:2 * i + 2, :], x1[:, 2 * i:2 * i + 2, :],
                        second[:, i % 2, :].rearrange("p (t d) -> p t d", t=2), ALU.add).then_inc(x1_ready, 1)
                elif kind == "fb":
                    half, ft = a
                    pool.wait_ge(dense_free[bank], done(f"bank{bank}"))
                    nc.gpsimd.tensor_tensor(hid[:, ft, :], hid[:, ft, :], second[:, ft % 2, :],
                                            ALU.add).then_inc(hid_ready, 1)
                elif kind == "w":
                    half, t = a
                    pool.wait_ge(dense_free[bank], done(f"bank{bank}") + 1)
                    nc.gpsimd.tensor_tensor(ob[:, t % 2, :], ob[:, t % 2, :], x1[:, 4 * half + t, :],
                                            ALU.add).then_inc(out_ready, 1)

            walk(pool, NB, run)

        @block.tensor
        def _(pe):
            def setup(i, db, db_b):
                if i == 0:
                    pe.wait_ge(consts_ready, 9)
                    pe.wait_ge(setup_chain, 3)
                    for k in range(KC):
                        last = nc.tensor.transpose(db[:, k * NB:(k + 1) * NB], c_sil[0:NB, k * P:(k + 1) * P],
                                                   ident[0:NB, 0:NB])
                elif i == 1:
                    pe.wait_ge(wmod_in, 16)
                    for n, piece in enumerate((0, 1, 2, 3, 6, 7, 8, 9)):
                        for k in range(KC):
                            last = nc.tensor.matmul(db[:, n * NB:(n + 1) * NB],
                                                    wmod_sb[:, k, piece * P:(piece + 1) * P], cond_t[:, k, :],
                                                    start=(k == 0), stop=(k == KC - 1))
                elif i == 2:
                    for n, piece in enumerate((2, 5)):
                        for k in range(KC):
                            last = nc.tensor.matmul(db[0:NB, n * D:(n + 1) * D], cond_t[:, k, :],
                                                    wmod_sb[:, k, piece * D:(piece + 1) * D],
                                                    start=(k == 0), stop=(k == KC - 1))
                elif i <= 4:
                    pe.wait_ge(weights_in, W_IN)
                    for n in range(2):
                        for t in range(KC):
                            last = nc.tensor.matmul(db[0:R, n * D + t * P:n * D + (t + 1) * P],
                                                    b_raw[:, 2 * (i - 3) + n, t, :], ident[:, :],
                                                    start=True, stop=True)
                elif i <= 8:
                    m = i - 5
                    for k in range(KC):
                        for t in range(KC):
                            o = db[:, k * D + t * P:k * D + (t + 1) * P]
                            nc.tensor.matmul(o, w_raw[:, m, t, k * P:(k + 1) * P], ident[:, :],
                                             start=True, stop=False)
                            last = nc.tensor.matmul(o, a_pad[:, m, k * P:(k + 1) * P],
                                                    bt_pad[:, m, t * P:(t + 1) * P], start=False, stop=True)
                elif i <= 12:
                    k, half = divmod(i - 9, 2)
                    for t in range(4):
                        last = nc.tensor.transpose(db[:, t * P:(t + 1) * P],
                                                   wi_raw[:, 4 * half + t, k * P:(k + 1) * P], ident[:, :])
                elif i <= 16:
                    for n in range(2):
                        for t in range(KC):
                            ft = 2 * (i - 13) + n
                            last = nc.tensor.transpose(db[:, n * D + t * P:n * D + (t + 1) * P],
                                                       wo_raw[:, t, ft * P:(ft + 1) * P], ident[:, :])
                elif i == 17:
                    pe.wait_ge(expert_in, 16 * (1 + E))
                    for k in range(KC):
                        last = nc.tensor.transpose(db[:, k * 32:(k + 1) * 32], r_raw[0:32, k * P:(k + 1) * P],
                                                   ident[0:32, 0:32])
                elif i == 18:
                    pe.wait_ge(setup_chain, 11)
                    for t in range(FT):
                        last = nc.tensor.transpose(db_b[0:KS, t * P:(t + 1) * P],
                                                   eb_w[:, t].rearrange("p s n -> p (s n)"), ident_b[:, :])
                else:
                    last = nc.tensor.matmul(db[:, 0:P], ident_b[:, :], causal_b[:, :], start=True, stop=True)
                return last

            def turned(db, f):
                for t in range(4):
                    last = nc.tensor.transpose(db[:, t * P:(t + 1) * P], f(t), ident[:, :])
                return last

            def run(step, done, it, bank):
                kind, *a = step
                db, db_b = dense_bank(bank)
                if kind == "mx":
                    slot, h0, heads, qt, chunk = a
                    n = max_keys(qt, chunk)
                    k0 = chunk * HB
                    bank_m = max_steps().index(tuple(a[1:])) % 2
                    after(pe, max_free, done("mx") - 1)
                    pe.wait_ge(stack_in[slot], done(f"rs{slot}") * (2 * SPLIT * 16))
                    for j in range(heads):
                        last = nc.tensor.matmul(mxs[:, bank_m, j * n:(j + 1) * n],
                                                q_st[0:KS, slot, h0 + j, qt * P:(qt + 1) * P],
                                                k_st[0:KS, slot, h0 + j, k0:k0 + n], start=True, stop=True)
                        if qt // 4 == chunk:
                            last = nc.tensor.matmul(mxs[:, bank_m, (j + 1) * n - P:(j + 1) * n], ident_b[:, :],
                                                    causal_b[:, :], start=False, stop=True, skip_group_check=True)
                    last.then_inc(max_full, 1)
                elif kind == "qk":
                    slot, ch, kt, j = a
                    q0 = max(kt * P, ch * HB)
                    n = (ch + 1) * HB - q0
                    if (ch, kt, j) == (*UNITS[0], 0):
                        pe.wait_ge(m_row_in, done("nm") * (HG * 16))
                    after(pe, exp_done, done("qk") - 2)
                    nc.tensor.matmul(st[:, (UNITS.index((ch, kt)) * HG + j) % 3, 0:n],
                                     k_st[0:KS + 2, slot, j, kt * P:(kt + 1) * P],
                                     q_st[0:KS + 2, slot, j, q0:q0 + n], start=True, stop=True
                                     ).then_inc(scores_ready, 1)
                elif kind == "pv":
                    slot, ch, kt = a
                    q0 = max(kt * P, ch * HB)
                    n = (ch + 1) * HB - q0
                    par = UNITS.index((ch, kt)) % 2
                    if kt == 0:
                        after(pe, ov_free, done("ov"))
                        pe.wait_ge(vg_ready, done("vg"))
                    pe.wait_ge(exp_done, HG * (done("pv") + 1))
                    if kt // 4 == ch:
                        pe.wait_ge(masked, done("pv diagonal") + 1)
                    for j in range(HG):
                        last = nc.tensor.matmul(ov[32 * j:32 * j + 32, HB - n:HB], v_g[:, slot, kt, j, :],
                                                probs[:, par, j, 0:n],
                                                start=(kt == 0), stop=(kt == 4 * ch + 3))
                    last.then_inc(pv_done, 1)
                elif kind == "fb":
                    half, ft = a
                    pe.wait_ge(relu_done, done("fb") + 1)
                    nc.tensor.matmul(db[:, :], b_stack[0:KS, ft * P:(ft + 1) * P],
                                     low_st[0:KS, 1, half * HB:(half + 1) * HB], start=False, stop=True,
                                     skip_group_check=True).then_inc(dense_full, 1)
                elif kind in DENSE:
                    if step[0:2] in (("su", 1), ("su", 5), ("ct", 0), ("op", 0)) or kind in ("rt", "rx") or step in (
                            ("pj", "q", 0, 0), ("fa", 0, 0)):
                        evacuated(pe, done)
                    else:
                        after(pe, dense_free[bank], done(f"bank{bank}"))
                    if kind == "su":
                        last = setup(a[0], db, db_b)
                    elif kind == "t1":
                        k, half = divmod(a[0], 2)
                        pe.wait_ge(norm1_ready, done("ln1"))
                        last = turned(db, lambda t: xin[:, 4 * half + t, k * P:(k + 1) * P])
                    elif kind == "t2":
                        k, half = divmod(a[0], 2)
                        pe.wait_ge(norm2_ready, done("ln2"))
                        last = turned(db, lambda t: x2n[:, 4 * half + t, k * P:(k + 1) * P])
                    elif kind == "ct":
                        k, half = divmod(a[0], 2)
                        last = turned(db, lambda t: ctx_n[:, 4 * half + t, k * P:(k + 1) * P])
                    elif kind == "ce":
                        pe.wait_ge(ov_free, done("ov"))
                        last = turned(db, lambda t: o_sb[:, a[1], t * P:(t + 1) * P])
                    elif kind == "rb":
                        pe.wait_ge(route_ready, done("ro"))
                        last = turned(db, lambda t: ratio_w[:, 4 * a[0] + t, :])
                    elif kind == "mt":
                        pe.wait_ge(route_ready, done("ro"))
                        for t in range(T):
                            last = nc.tensor.transpose(db_b[0:KS, t * P:(t + 1) * P],
                                                       low_w[:, a[0], t].rearrange("p s n -> p (s n)"), ident_b[:, :])
                    elif kind == "nm":
                        pe.wait_ge(negm_split, done("ms"))
                        for t in range(T):
                            last = nc.tensor.transpose(db_b[0:2 * HG, t * P:(t + 1) * P],
                                                       m_w[:, t].rearrange("p j s -> p (j s)"), ident_b[:, :])
                    elif kind == "pj":
                        which, ot, half = a
                        for k in range(KC):
                            last = nc.tensor.matmul(db[:, :], w_t[:, WNAMES.index(which), k, ot * P:(ot + 1) * P],
                                                    h_t[:, k, half * HB:(half + 1) * HB],
                                                    start=(k == 0), stop=(k == KC - 1))
                    elif kind in ("vp", "op"):
                        src, m = (h_t, 2) if kind == "vp" else (c_t, 3)
                        for n in range(2):
                            t = 2 * a[0] + n
                            for k in range(KC):
                                last = nc.tensor.matmul(db[:, n * D:(n + 1) * D], src[:, k, t * P:(t + 1) * P],
                                                        w_t[:, m, k, :], start=(k == 0), stop=(k == KC - 1))
                    elif kind == "rt":
                        for k in range(KC):
                            for j in range(4):
                                last = nc.tensor.matmul(db[32 * j:32 * j + 32, 0:D], rout_t[:, k, :],
                                                        c_t[:, k, j * D:(j + 1) * D],
                                                        start=(k == 0), stop=(k == KC - 1))
                    elif kind == "rx":
                        for s in range(2):
                            last = nc.tensor.transpose(db[:, s * P:(s + 1) * P], rout_sb[:, s * P:(s + 1) * P],
                                                       ident[:, :])
                    elif kind == "fa":
                        half, ft = a
                        for k in range(KC):
                            nc.tensor.matmul(db[:, :], wi_t[:, k, ft * P:(ft + 1) * P],
                                             c_t[:, k, half * HB:(half + 1) * HB], start=(k == 0), stop=False)
                        last = nc.tensor.matmul(db[:, :], b_stack[0:KS, ft * P:(ft + 1) * P],
                                                low_st[0:KS, 0, half * HB:(half + 1) * HB], start=False, stop=True)
                        last.then_inc(base_full, 1)
                        return
                    elif kind == "w":
                        half, t = a
                        pe.wait_ge(hid_ready, done("fb"))
                        for ft in range(FT):
                            last = nc.tensor.matmul(db[:, 0:D], hid[:, ft, t * P:(t + 1) * P], wo_t[:, ft, :],
                                                    start=(ft == 0), stop=(ft == FT - 1))
                    last.then_inc(dense_full, 1)

            walk(pe, NB, run)

        @block.scalar
        def _(act):
            def setup(i, db, db_b):
                if i == 0:
                    act.wait_ge(cond_in, 16)
                    nc.scalar.activation(c_sig[0:NB, :], c_raw[0:NB, :], ACT.Exp, scale=-1.0).then_inc(cond_exp, 1)
                act.wait_ge(dense_full, i + 1)
                if i == 0:
                    return nc.scalar.copy(cond_t, db[:, 0:KC * NB].rearrange("p (k b) -> p k b", k=KC))
                if i == 1:
                    return nc.scalar.copy(mod_t[:, :, :].rearrange("p b n -> p n b"),
                                          db[:, 0:8 * NB].rearrange("p (n b) -> p n b", b=NB))
                if i == 2:
                    return nc.scalar.copy(gate_raw[0:NB, :], db[0:NB, :])
                if i <= 4:
                    return nc.scalar.mul(bt_pad[0:R, 2 * (i - 3):2 * (i - 3) + 2, :],
                                         db[0:R, :].rearrange("p (m d) -> p m d", m=2), LORA_SCALE)
                if i <= 8:
                    return nc.scalar.copy(w_t[:, i - 5, :, :], db[:, :].rearrange("p (k d) -> p k d", k=KC))
                if i <= 12:
                    k, half = divmod(i - 9, 2)
                    return nc.scalar.copy(wi_t[:, k, half * HB:(half + 1) * HB], db[:, :])
                if i <= 16:
                    return nc.scalar.copy(wo_t[:, 2 * (i - 13):2 * (i - 13) + 2, :],
                                          db[:, :].rearrange("p (k d) -> p k d", k=2))
                if i == 17:
                    return nc.scalar.copy(rout_t[:, :, :], db[:, 0:KC * 32].rearrange("p (k n) -> p k n", k=KC))
                if i == 18:
                    return nc.scalar.copy(b_stack[0:KS, :], db_b[0:KS, :])
                return nc.scalar.copy(rest[:, 0, 0:P], db[:, 0:P])

            def run(step, done, it, bank):
                kind, *a = step
                db, db_b = dense_bank(bank)
                if kind == "qk":
                    slot, ch, kt, j = a
                    n = (ch + 1) * HB - max(kt * P, ch * HB)
                    par = UNITS.index((ch, kt)) % 2
                    if j == 0:
                        after(act, pv_done, done("pv"))
                    act.wait_ge(scores_ready, done("qk") + 1)
                    nc.scalar.activation(probs[:, par, j, 0:n], st[:, (UNITS.index((ch, kt)) * HG + j) % 3, 0:n],
                                         ACT.Exp, scale=SCORE_SCALE).then_inc(exp_done, 1)
                    return
                if kind == "ov":
                    act.wait_ge(pv_done, done("pv"))
                    nc.scalar.copy(o_sb[:, a[0], :], ov[:, :]).then_inc(ov_free, 1)
                    return
                if kind == "ro":
                    act.wait_ge(route_diff, done("ro") + 1)
                    nc.scalar.activation(rv[:, 1], rv[:, 0], ACT.Exp).then_inc(route_exp, 1)
                    return
                if kind == "su":
                    setup(a[0], db, db_b).then_inc(dense_free[bank], 1)
                    if a[0] == 5:
                        act.wait_ge(setup_chain, 17)
                        act.dma_start(gates_d, gate_raw[0:NB, :]).then_inc(gates_out, 16)
                    return
                if kind not in ("t1", "t2", "pj", "vp", "ct", "rt", "mt", "rb", "fa", "nm"):
                    return
                if kind == "fa":
                    half, ft = a
                    act.wait_ge(base_full, done("fa") + 1)
                    nc.scalar.activation(hid[:, ft, :], db[:, :], ACT.Relu).then_inc(relu_done, 1)
                    return
                act.wait_ge(dense_full, done("full") + 1)
                if kind in ("t1", "t2"):
                    k, half = divmod(a[0], 2)
                    dst, mod = (h_t, mod1) if kind == "t1" else (c_t, mod2)
                    nc.scalar.activation(dst[:, k, half * HB:(half + 1) * HB], db[:, :], ACT.Identity,
                                         scale=mod[:, 2 + k:3 + k], bias=mod[:, k:k + 1]).then_inc(dense_free[bank], 1)
                elif kind == "pj":
                    which, ot, half = a
                    dst = (q_part if which == "q" else k_part)[:, ot, :, half * HB:(half + 1) * HB]
                    if isinstance(it, int) and it < 0:
                        act.wait_ge(gates_out, 16)
                    after(act, parts_out[ot], done(f"ps{ot}") * (2 * 16))
                    nc.scalar.copy(dst[:, 0, :], db[:, :]).then_inc(part1_ready, 1)
                elif kind == "vp":
                    after(act, vg_ready, done("vg"))
                    nc.scalar.copy(v_st[:, 2 * a[0]:2 * a[0] + 2, :],
                                   db[:, :].rearrange("p (t d) -> p t d", t=2)).then_inc(dense_free[bank], 1)
                elif kind == "ct":
                    k, half = divmod(a[0], 2)
                    nc.scalar.copy(c_t[:, k, half * HB:(half + 1) * HB], db[:, :]).then_inc(dense_free[bank], 1)
                elif kind == "rt":
                    nc.scalar.copy(rout_sb[:, :], db[:, 0:D]).then_inc(dense_free[bank], 1)
                elif kind == "mt":
                    nc.scalar.copy(low_st[0:KS, a[0], :], db_b[0:KS, :]).then_inc(dense_free[bank], 1)
                elif kind == "rb":
                    nc.scalar.copy(ratio_b[:, a[0], :], db[:, :]).then_inc(dense_free[bank], 1)
                elif kind == "nm":
                    nc.scalar.copy(m_row[:, :], db_b[0:2 * HG, :]).then_inc(dense_free[bank], 1)
                    act.wait_ge(dense_free[bank], done(f"bank{bank}") + 1)
                    for j in range(HG):
                        act.dma_start(q_st[KS:KS + 2, a[0], j, :], m_row[2 * j:2 * j + 2, :]).then_inc(m_row_in, 16)

            walk(act, NB, run)

        @block.vector
        def _(dve):
            links = {"setup": 0}

            def setup_link(ins):
                links["setup"] += 1
                ins.then_inc(setup_chain, 1)
                dve.wait_ge(setup_chain, links["setup"])

            def setup_before():
                nc.vector.memset(k_st[KS:KS + 2, :, :, :], 1.0).then_inc(consts_ready, 1)
                dve.wait_ge(cond_exp, 1)
                setup_link(nc.vector.tensor_scalar_add(c_sig[0:NB, :], c_sig[0:NB, :], 1.0))
                setup_link(nc.vector.reciprocal(c_sig[0:NB, :], c_sig[0:NB, :]))
                setup_link(nc.vector.tensor_tensor(c_sil[0:NB, :], c_sig[0:NB, :], c_raw[0:NB, :], ALU.mult))
                dve.wait_ge(expert_in, 16 * (1 + E))
                setup_link(nc.vector.tensor_copy(eb_w[:, :, 0, :], eb_raw))
                setup_link(nc.vector.tensor_tensor(eb_rest, eb_raw, eb_w[:, :, 0, :], ALU.subtract))
                setup_link(nc.vector.tensor_copy(eb_w[:, :, 1, :], eb_rest))
                setup_link(nc.vector.tensor_tensor(eb_w[:, :, 4, :], eb_rest, eb_w[:, :, 1, :], ALU.subtract))
                setup_link(nc.vector.tensor_copy(eb_w[:, :, 2, :], eb_w[:, :, 0, :]))
                setup_link(nc.vector.tensor_copy(eb_w[:, :, 3, :], eb_w[:, :, 1, :]))
                setup_link(nc.vector.tensor_copy(eb_w[:, :, 5, :], eb_w[:, :, 0, :]))
                setup_link(nc.vector.memset(negm[:, :, :], 0.0))

            def setup_gates():
                dve.wait_ge(dense_free[0], 2)
                dve.wait_ge(dense_free[1], 1)
                setup_link(nc.vector.tensor_scalar_add(mod_t[:, :, 2:4], mod_t[:, :, 2:4], 1.0))
                setup_link(nc.vector.tensor_scalar_add(mod_t[:, :, 6:8], mod_t[:, :, 6:8], 1.0))
                setup_link(nc.vector.tensor_scalar(gate_sgn[0:NB, :], gate_raw[0:NB, :], 0.0, 2.0,
                                                   ALU.is_ge, ALU.mult))
                setup_link(nc.vector.scalar_tensor_tensor(
                    out=gate_abs[0:NB, :], in0=gate_raw[0:NB, :], scalar=-1.0, in1=gate_raw[0:NB, :],
                    op0=ALU.mult, op1=ALU.max))
                setup_link(nc.vector.tensor_scalar(gate_abs[0:NB, :], gate_abs[0:NB, :], GATE_MIN, None, ALU.max))
                setup_link(nc.vector.scalar_tensor_tensor(
                    out=gate_raw[0:NB, :], in0=gate_sgn[0:NB, :], scalar=-1.0, in1=gate_abs[0:NB, :],
                    op0=ALU.add, op1=ALU.mult))

            def layer_norm(src, dst, n, ready):
                k = [0]

                def link(ins):
                    k[0] += 1
                    ins.then_inc(norm_chain, 1)
                    dve.wait_ge(norm_chain, n * NORM_LINKS + k[0])

                for t in range(T):
                    last = nc.vector.bn_stats(stats[:, t, :], src[:, t, :])
                    k[0] += 1
                    last.then_inc(norm_chain, 1)
                dve.wait_ge(norm_chain, n * NORM_LINKS + k[0])
                nc.vector.memset(fence[:, 3:4], 0.0)
                for t in range(T):
                    last = nc.vector.bn_aggr(mv[:, t, :], stats[:, t, :])
                    k[0] += 1
                    last.then_inc(norm_chain, 1)
                dve.wait_ge(norm_chain, n * NORM_LINKS + k[0])
                var, y, b, sq = (nt[:, i, :] for i in range(4))
                link(nc.vector.tensor_scalar_add(var, mv[:, :, 1], LN_EPS))
                link(nc.vector.tensor_scalar(b.bitcast(I32), var.bitcast(I32), 1, None, ALU.arith_shift_right))
                link(nc.vector.tensor_scalar(y.bitcast(I32), b.bitcast(I32), -1.0, RSQRT_SEED, ALU.mult, ALU.add))
                for _ in range(3):
                    link(nc.vector.tensor_tensor(sq, y, y, ALU.mult))
                    link(nc.vector.scalar_tensor_tensor(out=b, in0=sq, scalar=-0.5, in1=var, op0=ALU.mult,
                                                        op1=ALU.mult))
                    link(nc.vector.scalar_tensor_tensor(out=y, in0=b, scalar=1.5, in1=y, op0=ALU.add,
                                                        op1=ALU.mult))
                assert k[0] == NORM_LINKS
                for t in range(T):
                    last = nc.vector.tensor_scalar(dst[:, t, :], src[:, t, :], mv[:, t, 0:1], y[:, t:t + 1],
                                                   ALU.subtract, ALU.mult)
                last.then_inc(ready, 1)

            def route(n, it):
                k = [0]

                def link(ins):
                    k[0] += 1
                    ins.then_inc(route_chain, 1)
                    dve.wait_ge(route_chain, n * ROUTE_LINKS + k[0])

                d, ex, v, sel1, d2, v2, sel2, wt = (rv[:, i] for i in range(8))
                top, s1, m2, s2, total, w1, r = (rs_[:, i] for i in range(7))

                def wide(s):
                    return s.unsqueeze(2).broadcast_to([P, T, E])

                link(nc.vector.tensor_tensor(wt, lg[:, :, 0:E], bg_b[:, :].unsqueeze(1).broadcast_to([P, T, E]),
                                             ALU.add))
                link(nc.vector.tensor_reduce(top, wt, axis=AX.X, op=ALU.max))
                nc.vector.tensor_tensor(d, wt, wide(top), ALU.subtract).then_inc(route_diff, 1)
                dve.wait_ge(route_diff, n + 1)
                link(nc.vector.scalar_tensor_tensor(out=v, in0=d, scalar=0.0, in1=prio[:, :, :],
                                                    op0=ALU.is_equal, op1=ALU.mult))
                link(nc.vector.tensor_reduce(s1, v, axis=AX.X, op=ALU.max))
                link(nc.vector.tensor_tensor(sel1, v, wide(s1), ALU.is_equal))
                link(nc.vector.scalar_tensor_tensor(out=d2, in0=sel1, scalar=BIG, in1=d, op0=ALU.mult, op1=ALU.add))
                link(nc.vector.tensor_reduce(m2, d2, axis=AX.X, op=ALU.max))
                link(nc.vector.tensor_tensor(d2, d2, wide(m2), ALU.subtract))
                link(nc.vector.scalar_tensor_tensor(out=v2, in0=d2, scalar=0.0, in1=prio[:, :, :],
                                                    op0=ALU.is_equal, op1=ALU.mult))
                link(nc.vector.tensor_reduce(s2, v2, axis=AX.X, op=ALU.max))
                link(nc.vector.tensor_tensor(sel2, v2, wide(s2), ALU.is_equal))
                dve.wait_ge(route_exp, n + 1)
                link(nc.vector.tensor_reduce(total, ex, axis=AX.X, op=ALU.add))
                link(nc.vector.reciprocal(w1, total))
                link(nc.vector.tensor_tensor(wt, ex, sel2, ALU.mult))
                link(nc.vector.tensor_reduce(r, wt, axis=AX.X, op=ALU.add))
                link(nc.vector.tensor_copy(ratio_w[:, :, :], r.unsqueeze(2).broadcast_to([P, T, P])))
                link(nc.vector.tensor_tensor(d2, sel2, sel1, ALU.subtract))
                low = lg[:, :, E:E + DH].rearrange("p t (e r) -> p t e r", e=E)
                for i, mask in enumerate((sel1, d2)):
                    last = nc.vector.tensor_tensor(
                        lowf[:, i].rearrange("p t (e r) -> p t e r", e=E), low,
                        mask.unsqueeze(3).broadcast_to([P, T, E, RK]), ALU.mult)
                    if i == 0:
                        k[0] += 1
                        last.then_inc(route_chain, 1)
                link(last)
                full = lowf[:, :, :, :].rearrange("p v t n -> p (v t) n")
                left = lowr[:, :, :, :].rearrange("p v t n -> p (v t) n")
                stack = low_w[:, :, :, :, :].rearrange("p v t s n -> p (v t) s n")
                nvt = 2 * T
                link(nc.vector.tensor_copy(stack[:, :, 0:2, :], full.unsqueeze(2).broadcast_to([P, nvt, 2, DH])))
                nc.vector.tensor_copy(stack[:, :, 4, :], full).then_inc(route_chain, 1)
                k[0] += 1
                link(nc.vector.tensor_tensor(left, full, stack[:, :, 0, :], ALU.subtract))
                link(nc.vector.tensor_copy(stack[:, :, 2:4, :], left.unsqueeze(2).broadcast_to([P, nvt, 2, DH])))
                assert k[0] == ROUTE_LINKS, k[0]
                nc.vector.tensor_tensor(stack[:, :, 5, :], left, stack[:, :, 2, :],
                                        ALU.subtract).then_inc(route_ready, 1)

            def run(step, done, it, bank):
                kind, *a = step
                db, db_b = dense_bank(bank)
                if kind == "su":
                    if a[0] == 0:
                        setup_before()
                    elif a[0] == 3:
                        setup_gates()
                        dve.wait_ge(consts_ready, 9)
                elif kind == "ln1":
                    dve.wait_ge(xin_in, 16 * (done("ln1") + 1))
                    nc.vector.tensor_copy(mod1[:, :], mod_t[:, it + 1, 0:4] if isinstance(it, int)
                                          else mod_t[:, bass.ds(it + 1, 1), 0:4].rearrange("p b n -> p (b n)"))
                    layer_norm(xin, xin, done("ln1") + done("ln2"), norm1_ready)
                elif kind == "ln2":
                    dve.wait_ge(x1_ready, done("op"))
                    nc.vector.tensor_copy(mod2[:, :], mod_t[:, it - 1, 4:8] if isinstance(it, int)
                                          else mod_t[:, bass.ds(it - 1, 1), 4:8].rearrange("p b n -> p (b n)"))
                    layer_norm(x1, x2n, done("ln1") + done("ln2"), norm2_ready)
                elif kind == "ro":
                    evacuated(dve, done)
                    route(done("ro"), it)
                elif kind == "mx":
                    slot, h0, heads, qt, chunk = a
                    n = max_keys(qt, chunk)
                    dve.wait_ge(max_full, done("mx") + 1)
                    src = mxs[:, max_steps().index(tuple(a[1:])) % 2, 0:heads * n].rearrange("p (j k) -> p j k", k=n)
                    dst = negm[:, qt] if chunk == qt // 4 else negm_left[:, qt - 4]
                    nc.vector.tensor_reduce(dst[:, h0:h0 + heads], src, axis=AX.X, op=ALU.max,
                                            negate=True).then_inc(max_free, 1)
                elif kind == "vg":
                    g = a[0]
                    if g == 0:
                        evacuated(dve, done)
                    after(dve, pv_done, done("pv"))
                    nc.vector.tensor_copy(
                        v_g[:, g % 2, :, :, 0:DH],
                        v_st[:, :, HG * DH * g:HG * DH * (g + 1)].rearrange("p t (j d) -> p t j d", j=HG)
                    ).then_inc(vg_ready, 1)
                elif kind == "ms":
                    dve.wait_ge(max_free, done("mx"))
                    nc.vector.tensor_tensor(negm[:, 4:T, :], negm[:, 4:T, :], negm_left[:, :, :],
                                            ALU.min).then_inc(negm_ready, 1)
                    dve.wait_ge(negm_ready, done("ms") + 1)
                    nc.vector.tensor_copy(m_w[:, :, :, 0], negm[:, :, :]).then_inc(negm_hi, 1)
                    dve.wait_ge(negm_hi, done("ms") + 1)
                    nc.vector.tensor_tensor(m_w[:, :, :, 1], negm[:, :, :], m_w[:, :, :, 0],
                                            ALU.subtract).then_inc(negm_split, 1)
                elif kind == "pj":
                    which, ot, half = a
                    dst = (q_part if which == "q" else k_part)[:, ot, :, half * HB:(half + 1) * HB]
                    par = 0 if which == "q" else 1
                    dve.wait_ge(part1_ready, done("pj") + 1)
                    after(dve, part3_ready, done("pj") - 1)
                    nc.vector.tensor_tensor(rest[:, par, :], db[:, :], dst[:, 0, :],
                                            ALU.subtract).then_inc(dense_free[bank], 1)
                    dve.wait_ge(dense_free[bank], done(f"bank{bank}") + 1)
                    nc.vector.tensor_copy(dst[:, 1, :], rest[:, par, :]).then_inc(part2_ready, 1)
                elif kind == "ce":
                    g, ch = a
                    dve.wait_ge(dense_full, done("full") + 1)
                    o = db[:, :].rearrange("p (q j e) -> p q j e", q=4, j=HG)
                    nc.vector.reciprocal(rsum[:, :, :], o[:, :, :, DH]).then_inc(rsum_ready, 1)
                    dve.wait_ge(rsum_ready, done("ce") + 1)
                    nc.vector.tensor_tensor(
                        ctx_n[:, 4 * ch:4 * ch + 4, HG * DH * g:HG * DH * (g + 1)].rearrange(
                            "p q (j d) -> p q j d", j=HG),
                        o[:, :, :, 0:DH], rsum[:, :, :].unsqueeze(3).broadcast_to([P, 4, HG, DH]),
                        ALU.mult).then_inc(dense_free[bank], 1)
                elif kind == "op":
                    i = a[0]
                    if i == 0:
                        dve.wait_ge(gates_in, 16 * done("xl"))
                    dve.wait_ge(dense_full, done("full") + 1)
                    if i >= 2:
                        dve.wait_ge(x1_ready, done("op") - 1)
                    nc.vector.tensor_tensor(
                        second[:, i % 2, :].rearrange("p (t d) -> p t d", t=2),
                        db[:, :].rearrange("p (t d) -> p t d", t=2),
                        gates_b[:, 0:D].unsqueeze(1).broadcast_to([P, 2, D]), ALU.mult).then_inc(dense_free[bank], 1)
                elif kind == "rx":
                    dve.wait_ge(dense_full, done("full") + 1)
                    for s in range(2):
                        last = nc.vector.tensor_copy(
                            lg[:, :, :].rearrange("p (j s) n -> p s j n", s=2)[:, s],
                            db[:, s * P:(s + 1) * P].rearrange("p (j n) -> p j n", j=4)[:, :, 0:E + DH])
                    last.then_inc(dense_free[bank], 1)
                elif kind == "fb":
                    half, ft = a
                    dve.wait_ge(dense_full, done("full") + 1)
                    if (half, ft) >= (0, 2):
                        dve.wait_ge(hid_ready, done("fb") - 1)
                    nc.vector.scalar_tensor_tensor(out=second[:, ft % 2, :], in0=db[:, :], scalar=0.0,
                                                   in1=ratio_b[:, half, :], op0=ALU.max,
                                                   op1=ALU.mult).then_inc(dense_free[bank], 1)
                elif kind == "w":
                    half, t = a
                    dve.wait_ge(dense_full, done("full") + 1)
                    dve.wait_ge(out_done[t % 2], 16 * (done(f"w{t % 2}") + 1))
                    nc.vector.scalar_tensor_tensor(out=ob[:, t % 2, :], in0=db[:, 0:D],
                                                   scalar=rs_[:, 5, 4 * half + t:4 * half + t + 1],
                                                   in1=gates_b[:, D:2 * D], op0=ALU.mult,
                                                   op1=ALU.mult).then_inc(dense_free[bank], 1)

            walk(dve, NB, run)


_INS = ["L0_attn_x", "L0_attn_wq", "L0_attn_aq", "L0_attn_bq", "L0_attn_wk", "L0_attn_ak", "L0_attn_bk",
        "L0_attn_wv", "L0_attn_av", "L0_attn_bv", "L0_attn_wo", "L0_attn_ao", "L0_attn_bo", "L0_ffn_Wg",
        "L0_ffn_bg", "L0_ffn_Wi", "L0_ffn_Wo", "L0_ffn_A", "L0_ffn_B", "L0_c", "L0_wmod"]


def kernel(**inputs):
    import numpy as np
    import concourse.bacc as bacc
    from concourse.bass_utils import run_bass_kernel_spmd

    nc = bacc.Bacc("TRN2", target_bir_lowering=False, num_devices=1)
    arrays, args = {}, []
    for name in _INS:
        a = np.ascontiguousarray(inputs[name])
        arrays[f"in_{name}"] = a
        args.append(nc.dram_tensor(f"in_{name}", a.shape, mybir.dt.from_np(a.dtype), kind="ExternalInput").ap())
    x = inputs["L0_attn_x"]
    args.append(nc.dram_tensor("out_x", x.shape, F32, kind="ExternalOutput").ap())
    adaln_block(nc, *args)
    r = run_bass_kernel_spmd(nc, [arrays], core_ids=[0])
    return r.results[0]["out_x"]
```

```python
from contextlib import ExitStack

import concourse.bass as bass
from concourse import mybir

F32 = mybir.dt.float32
BF16 = mybir.dt.bfloat16
I32 = mybir.dt.int32
ALU = mybir.AluOpType
ACT = mybir.ActivationFunctionType
AX = mybir.AxisListType

P = 128
DH = 16
HG = 4
SPLIT = 6
Q_PARTS = (0, 0, 1, 1, 0, 2)
K_PARTS = (0, 1, 0, 1, 2, 0)
KS = SPLIT * DH
BIG = -3.0e38
LN_EPS = 1e-5
RSQRT_SEED = float(0x5F3759DF)
GATE_MIN = 0.25

DENSE = frozenset("su t1 pj vp ct op t2 rt rx mt rb fa wa ce nm".split())
GOES_ON = {"fa": "fb", "wa": "w"}


def attention_units():
    return [(c, kt) for c in range(2) for kt in range(4 * (c + 1))]


UNITS = attention_units()
NU = len(UNITS)
GROUPS = 4
MAX_BANKS = 3
SCORE_BANKS = 2
NM_UNIT = NU - 3
VG_UNIT = 8
V_FREE = (GROUPS - 2) * NU + VG_UNIT + 1
V_NEEDED = (GROUPS - 1) * NU + VG_UNIT


def max_steps():
    steps = []
    for qt in range(7, -1, -1):
        if qt >= 4:
            steps += [(h, 1, qt, 0) for h in range(HG)]
        heads = {0: [4], 1: [2, 2] if qt < 4 else [2, 1, 1]}.get(qt % 4, [1] * HG)
        steps += [(sum(heads[:i]), n, qt, qt // 4) for i, n in enumerate(heads)]
    assert len(steps) % MAX_BANKS == 0
    return steps


def unit_queries(c, kt):
    q0 = max(kt * P, c * 512)
    return q0, (c + 1) * 512 - q0


def score_steps(slot, c, kt):
    n = unit_queries(c, kt)[1]
    heads = {128: 4, 256: 2}.get(n, 1)
    return [("qk", slot, c, kt, h, heads) for h in range(0, HG, heads)]


def max_keys(qt, chunk):
    return min((qt + 1) * P - chunk * 512, 512)


def pe_cost(step):
    if step[0] == "mx":
        _, _, _, heads, qt, chunk = step
        return (max_keys(qt, chunk) + P * (qt // 4 == chunk)) * heads / 2.4
    return {"ct": 300, "op": 1750, "t1": 300, "t2": 300, "rt": 1000, "rx": 200, "mt": 500, "rb": 300,
            "pj": 1750, "vp": 1750, "fa": 1950, "fb": 250, "wa": 1750, "w": 1750, "ce": 450, "nm": 850}.get(step[0], 0)


def body_plan(pre, post, lead):
    queue = []

    def put(unit, *steps):
        queue.extend((unit, (s,)) for s in steps)

    early = [("pj", w, ot, half) for ot in range(2) for half in range(2) for w in "qk"]
    early.insert(4, ("ps", 0))
    late = [("vp", i) for i in range(4)]
    if post:
        put(0, ("ce", GROUPS - 1, 1))
    if pre:
        put(0, ("ls1",))
    if post:
        put(0, *[("ct", i) for i in range(4)])
    if pre:
        put(1, ("ln1",))
    if post:
        put(1, *[("op", i) for i in range(4)])
    if pre:
        put(3, *[("t1", i) for i in range(4)], ("xin",))
        put(4, *early[:5])
    if post:
        put(9, ("ls2",), ("ln2",))
    if pre:
        put(11, *early[5:7])
    if post:
        put(11, *[("t2", i) for i in range(4)], ("rt",), ("rx",), ("ro",))
    if pre:
        put(13, *early[7:])
    if post:
        put(14, *[("mt", v) for v in range(2)], *[("rb", half) for half in range(2)])
        for half in range(2):
            for quad in hidden_quads(half):
                queue.append((8, quad))
                if half and pre:
                    put(V_FREE, late[quad[0][2] // 2])
            queue.extend((8, (("wa", half, t), ("w", half, t))) for t in range(4))
    elif pre:
        put(V_FREE, *late)
    unit_cost = [8 * 512 / 2.4 if kt < 4 * c else 8 * (512 - 128 * (kt % 4)) / 2.4 for c, kt in UNITS]
    row_maxima = [0, 3, 4, 4, 5, 5, 6, 6, 6, 0, 0, 0] if post else [0, 4, 4, 5, 6, 6, 5, 5, 4, 0, 0, 0]
    parts_left = pre
    fixed = 8 * pe_cost(("ce",)) + 4 * pe_cost(("nm",))
    total = GROUPS * (sum(unit_cost) + sum(pe_cost(("mx", 0, *s)) for s in max_steps())) + fixed
    total += sum(pe_cost(s) for _, q in queue for s in q)
    spent = 0.0
    plan = []
    if post:
        plan.append(("xl",))
    for u in range(GROUPS * NU):
        g, k = divmod(u, NU)
        c, kt = UNITS[k]
        more = lead or g < GROUPS - 1
        pinned = []
        if k == NM_UNIT and more:
            pinned.append(("nm", (g + 1) % 2))
        if k in (4, 0) and u > 0:
            pinned.append(("ce", g, 0) if k == 4 else ("ce", g - 1, 1))
        fillers = []
        first = sum(row_maxima[:k])
        mx = [("mx", (g + 1) % 2, *s) for s in max_steps()[first:first + row_maxima[k]]] if more else []
        spent += unit_cost[k] + sum(map(pe_cost, mx + pinned))
        goal = total * (u + 1) / (GROUPS * NU)
        while queue and queue[0][0] <= u:
            due = u == GROUPS * NU - 1 or u == V_NEEDED - 1 and any(s in late for _, q in queue for s in q)
            if spent + sum(map(pe_cost, queue[0][1])) / 2 > goal and not due:
                break
            fillers.append(queue[0][1])
            spent += sum(map(pe_cost, queue.pop(0)[1]))
        following = []
        if u + 1 < GROUPS * NU or lead:
            following = score_steps((u + 1) // NU % 2, *UNITS[(u + 1) % NU])
        if k == NU - 1 and (pre or g < 2):
            plan.append(("rs", g % 2, (g + 2) % GROUPS))
        fillers.insert(0 if k == NM_UNIT else (len(fillers) + 1) // 2, pinned)
        together = [s for q in fillers for s in q]
        length = sum(map(pe_cost, together)) or 1
        turns = [((i + 0.5) / len(following), 0, s) for i, s in enumerate(following)]
        turns += [((i + 0.35) / len(mx), 1, s) for i, s in enumerate(mx)]
        turns += [((sum(map(pe_cost, together[:i])) + pe_cost(s) / 2) / length, 2, s) for i, s in enumerate(together)]
        for _, n, s in sorted(turns, key=lambda turn: turn[:2]):
            plan.append(s)
            if n == 1 and s is mx[-1] and sum(row_maxima[:k + 1]) == len(max_steps()):
                plan.append(("ms",))
        if parts_left and u >= 2 * NU and not any(s in early for _, q in queue for s in q):
            plan.append(("ps", 1))
            parts_left = False
        plan.append(("pv", g % 2, c, kt))
        if kt == 4 * c + 3:
            plan.append(("ov", c))
        if k == VG_UNIT and more:
            plan.append(("vg", (g + 1) % GROUPS))
    assert not queue
    at = {s: i for i, s in enumerate(plan)}
    if pre:
        assert at["vp", 3] < at["vg", 0] and at["ps", 0] < at["rs", 0, 0] and at["ps", 1] < at["rs", 1, 1]
    return plan


def hidden_quads(half):
    return [(("fa", half, ft), ("fa", half, ft + 1), ("fb", half, ft), ("fb", half, ft + 1))
            for ft in range(0, 8, 2)]


def prologue_plan():
    pj = [[("pj", w, ot, half) for half in range(2) for w in "qk"] for ot in range(2)]
    plan = [("su", i) for i in range(N_PROJECTION_SETUP)]
    plan += [("ls1",), ("ln1",)] + [("t1", i) for i in range(4)] + [("xin",)]
    plan += pj[0] + [("ps", 0), ("rs", 0, 0), ("rs", 1, 1)]
    plan += [("vp", i) for i in range(4)] + [("vg", 0)]
    plan += pj[1][:3] + [("su", N_PROJECTION_SETUP)]
    beside = pj[1][3:] + [("su", i) for i in range(N_PROJECTION_SETUP + 1, N_SETUP)]
    mx = [("mx", 0, *s) for s in max_steps()]
    for i, s in enumerate(beside):
        plan += [s] + mx[4 * i:4 * i + 4]
    assert 4 * len(beside) >= len(mx)
    plan += [("ms",), ("ps", 1), ("nm", 0)] + score_steps(0, *UNITS[0])
    return plan


def epilogue_plan():
    plan = [("xl",), ("ce", GROUPS - 1, 1)] + [("ct", i) for i in range(4)] + [("op", i) for i in range(4)]
    plan += [("ls2",), ("ln2",)] + [("t2", i) for i in range(4)] + [("rt",), ("rx",), ("ro",)]
    plan += [("mt", v) for v in range(2)] + [("rb", half) for half in range(2)]
    for half in range(2):
        for quad in hidden_quads(half):
            plan += quad
        plan += [s for t in range(4) for s in (("wa", half, t), ("w", half, t))]
    return plan


N_PROJECTION_SETUP = 9
N_SETUP = 19


def tallied(step, bank):
    names = [step[0]]
    if step[0] in DENSE:
        names.append(f"bank{bank}")
    if step[0] in DENSE and step[0] not in GOES_ON or step[0] in GOES_ON.values():
        names.append("full")
    if step[0] == "pv" and step[2] == step[3] // 4:
        names.append("pv diagonal")
    if step[0] == "pv":
        names += ["scored"] * len(score_steps(*step[1:]))
    if step[0] == "qk" and step[2] == step[3] // 4 and step[4] + step[5] == HG:
        names.append("qk diagonal")
    if step[0] in ("rs", "ps"):
        names.append(f"{step[0]}{step[1]}")
    if step[0] == "w":
        names.append(f"w{step[2] % 2}")
    return names


def with_banks(plan, first):
    n, steps, open_at = first, [], {}
    for s in plan:
        bank = None
        if s[0] in DENSE:
            bank = n % 2
            n += 1
            if s[0] in GOES_ON:
                open_at[GOES_ON[s[0]], *s[1:]] = bank
        elif s in open_at:
            bank = open_at[s]
        steps.append((s, bank))
    return steps, n % 2


def walk(eng, batches, run, late=None):
    counts = {}
    bank_next = [0]

    def phase(plan, it, reg):
        first = bank_next[0]
        steps, bank_next[0] = with_banks(plan, first)
        assert reg is None or bank_next[0] == first
        per = {}
        for s, bank in steps:
            for n in tallied(s, bank):
                per[n] = per.get(n, 0) + 1
        here = {}
        held_back = []
        for s, bank in steps:
            def done(name, here=dict(here)):
                fixed = counts.get(name, 0) + here.get(name, 0)
                return fixed if reg is None or not per.get(name) else reg * per[name] + fixed
            if held_back and s[0] not in ("mx", "pv", "qk"):
                run(*held_back.pop())
            if s[0] == late:
                held_back.append((s, done, it, bank))
            else:
                run(s, done, it, bank)
                if held_back and s[0] == "mx":
                    run(*held_back.pop())
            for n in tallied(s, bank):
                here[n] = here.get(n, 0) + 1
        for n, m in per.items():
            counts[n] = counts.get(n, 0) + m * (1 if reg is None else batches - 2)

    phase(prologue_plan(), -1, None)
    phase(body_plan(pre=True, post=False, lead=True), 0, None)
    with eng.Fori(0, batches - 2) as reg:
        phase(body_plan(pre=True, post=True, lead=True), reg + 1, reg)
    phase(body_plan(pre=False, post=True, lead=False), batches - 1, None)
    phase(epilogue_plan(), batches, None)


def after(eng, sem, value):
    if not isinstance(value, int) or value > 0:
        eng.wait_ge(sem, value)


def held(eng, value):
    return value if isinstance(value, int) else eng.to_reg(value)


def adaln_block(nc, x, wq, aq, bq, wk, ak, bk, wv, av, bv, wo, ao, bo, Wg, bg, Wi, Wo, A, Bm, c, wmod, out):
    NB, S, D = x.shape
    R = aq.shape[0]
    F = Wi.shape[0]
    E, RK, _ = A.shape
    T = S // P
    KC = D // P
    FT = F // P
    HB = S // 2
    LORA_SCALE = 1.0 / R
    SCORE_SCALE = float(DH) ** -0.5
    assert (S, D, R, F, E * RK, NB) == (1024, 256, DH, 1024, DH, 8)

    x_t = x.rearrange("b (t p) d -> b p t d", p=P)
    out_t = out.rearrange("b (t p) d -> b t p d", p=P)

    with ExitStack() as ctx:
        def sb(name, shape, dt=F32):
            return ctx.enter_context(nc.sbuf_tensor(name, shape, dt))

        def sem(name):
            return ctx.enter_context(nc.semaphore(name))

        ident = sb("ident", [P, P])
        ident_b = sb("ident_b", [P, P], BF16)
        causal_b = sb("causal_b", [P, P], BF16)
        w_t = sb("w_t", [P, 4, KC, D])
        wi_t = sb("wi_t", [P, KC, F])
        wo_t = sb("wo_t", [P, FT, D])
        rout_t = sb("rout_t", [P, KC, 32])
        b_stack = sb("b_stack", [P, F], BF16)
        bg_b = sb("bg_b", [P, E])
        prio = sb("prio", [P, T, E])
        mod_t = sb("mod_t", [P, NB, 8])
        mod1 = sb("mod1", [P, 4])
        mod2 = sb("mod2", [P, 4])
        gates_b = sb("gates_b", [P, 2 * D])
        xin = sb("xin", [P, T, D])
        x1 = sb("x1", [P, T, D])
        h_t = sb("h_t", [P, KC, S])
        ctx_n = sb("ctx_n", [P, T, D])
        c_t = sb("c_t", [P, KC, S])
        v_st = sb("v_st", [P, T, D])
        v_g = sb("v_g", [P, 2, T, HG, 32])
        q_part = sb("q_part", [P, 2, 3, S], BF16)
        k_part = sb("k_part", [P, 2, 3, S], BF16)
        rest = sb("rest", [P, 2, HB])
        q_st = sb("q_st", [P, 2, HG, S], BF16)
        k_st = sb("k_st", [P, 2, HG, S], BF16)
        probs = sb("probs", [P, 2, HG, HB])
        o_sb = sb("o_sb", [P, 2, HB])
        hid = sb("hid", [P, FT, HB])
        second = sb("second", [P, 2, HB])
        ob = sb("ob", [P, 2, D])
        ratio_b = sb("ratio_b", [P, 2, HB])
        low_st = sb("low_st", [P, 2, S], BF16)
        low_w = sb("low_w", [P, 2, T, SPLIT, DH], BF16)
        rout_sb = sb("rout_sb", [P, D])
        m_row = sb("m_row", [8, S], BF16)
        negm = sb("negm", [P, T, HG])
        negm_left = sb("negm_left", [P, T - 4, HG])
        m_w = sb("m_w", [P, T, HG, 2], BF16)
        rsum = sb("rsum", [P, 4, HG])
        stats = sb("stats", [P, T, 6])
        fence = sb("fence", [P, 4])
        mv = sb("mv", [P, T, 2])
        nt = sb("nt", [P, 4, T])
        lg = sb("lg", [P, T, E + DH])
        rv = sb("rv", [P, 8, T, E])
        rs_ = sb("rs_", [P, 8, T])
        lowf = sb("lowf", [P, 2, T, DH])
        lowr = sb("lowr", [P, 2, T, DH])
        ratio_w = second[:, :, :].rearrange("p a (t n) -> p (a t) n", n=P)
        x2n = hid[:, :, :].rearrange("p a b -> p (a b)")[:, 0:T * D].rearrange("p (t d) -> p t d", t=T)

        hid_f = hid[:, :, :].rearrange("p a b -> p (a b)")
        wi_raw = hid_f[:, 0:FT * D].rearrange("p (t d) -> p t d", t=FT)
        wo_raw = hid_f[:, FT * D:2 * FT * D].rearrange("p (t f) -> p t f", t=KC)
        probs_f = probs[:, :, :, :].rearrange("p a b c -> p (a b c)")
        wmod_sb = probs_f[:, 0:KC * 6 * D].rearrange("p (k n) -> p k n", k=KC)
        a_pad = probs_f[:, KC * 6 * D:KC * 6 * D + 4 * D].rearrange("p (m d) -> p m d", m=4)
        qp_f = q_part[:, :, :, :].rearrange("p a b c -> p (a b c)").bitcast(F32)
        w_raw = qp_f[:, 0:4 * KC * D].rearrange("p (m t d) -> p m t d", m=4, t=KC)
        bt_pad = qp_f[:, 2048:2048 + 4 * D].rearrange("p (m d) -> p m d", m=4)
        kp_f = k_part[:, :, :, :].rearrange("p a b c -> p (a b c)").bitcast(F32)
        b_raw = kp_f[:, 0:128].rearrange("p (m t r) -> p m t r", m=4, t=KC)
        low_f = low_st[:, :, :].rearrange("p a b -> p (a b)").bitcast(F32)
        eb_raw = low_f[:, 0:FT * DH].rearrange("p (t n) -> p t n", t=FT)
        eb_rest = low_f[:, FT * DH:2 * FT * DH].rearrange("p (t n) -> p t n", t=FT)
        r_raw = low_f[:, 2 * FT * DH:2 * FT * DH + D]
        eb_w = low_st[:, 1, 0:FT * KS].rearrange("p (t s n) -> p t s n", t=FT, s=SPLIT)
        c_raw = kp_f[:, 1280:1536]
        c_sig = kp_f[:, 1536:1792]
        c_sil = kp_f[:, 1792:2048]
        cond_t = kp_f[:, 2048:2048 + KC * NB].rearrange("p (k b) -> p k b", k=KC)
        gate_raw = kp_f[:, 2304:2304 + 2 * D]
        gate_abs = o_sb[:, 0, :]
        gate_sgn = o_sb[:, 1, :]

        st = ctx.enter_context(nc.psum_tensor("st", [P, SCORE_BANKS, HB], F32))
        ov = ctx.enter_context(nc.psum_tensor("ov", [P, HB], F32))
        mxs = ctx.enter_context(nc.psum_tensor("mxs", [P, MAX_BANKS, HB], F32))
        dense = ctx.enter_context(nc.psum_tensor("dense", [P, 2, HB], F32))

        def dense_bank(bank):
            db = dense[:, bank or 0, :]
            return db, db.bitcast(BF16)

        of_group = [s[2:5] for u in UNITS for s in score_steps(0, *u)]
        assert len(of_group) % SCORE_BANKS == 0

        def score_bank(ch, kt, h0):
            return of_group.index((ch, kt, h0)) % SCORE_BANKS

        def evacuated(eng, done):
            for i in range(2):
                after(eng, dense_free[i], done(f"bank{i}"))

        q_d, k_d = (nc.dram_tensor(f"{w}_parts_scratch", [2, P, 3, S], BF16, kind="Internal").ap() for w in "qk")
        gates_d = nc.dram_tensor("gates_scratch", [NB, 2 * D], F32, kind="Internal").ap()

        projections_in = sem("projections_in")
        ffn_in = sem("ffn_in")
        cond_in = sem("cond_in")
        wmod_in = sem("wmod_in")
        expert_in = sem("expert_in")
        zeroed = sem("zeroed")
        consts_ready = sem("consts_ready")
        ones_ready = sem("ones_ready")
        gates_out = sem("gates_out")
        setup_chain = sem("setup_chain")
        cond_exp = sem("cond_exp")
        xin_in = sem("xin_in")
        x1_in = sem("x1_in")
        gates_in = sem("gates_in")
        norm1_ready = sem("norm1_ready")
        norm2_ready = sem("norm2_ready")
        norm_chain = sem("norm_chain")
        dense_full = sem("dense_full")
        dense_free = [sem(f"dense_free{i}") for i in range(2)]
        base_full = sem("base_full")
        relu_done = sem("relu_done")
        part1_ready = sem("part1_ready")
        rest_ready = sem("rest_ready")
        part2_ready = sem("part2_ready")
        part3_ready = sem("part3_ready")
        stack_in = [sem(f"stack_in{s}") for s in range(2)]
        parts_out = [sem(f"parts_out{i}") for i in range(2)]
        max_full = sem("max_full")
        max_free = sem("max_free")
        negm_split = sem("negm_split")
        negm_ready = sem("negm_ready")
        negm_hi = sem("negm_hi")
        m_row_in = sem("m_row_in")
        scores_ready = sem("scores_ready")
        exp_done = sem("exp_done")
        fenced = sem("fenced")
        masked = sem("masked")
        vg_ready = sem("vg_ready")
        pv_done = sem("pv_done")
        ov_free = sem("ov_free")
        rsum_ready = sem("rsum_ready")
        x1_ready = sem("x1_ready")
        route_chain = sem("route_chain")
        route_diff = sem("route_diff")
        route_exp = sem("route_exp")
        route_ready = sem("route_ready")
        hid_ready = sem("hid_ready")
        out_scaled = sem("out_scaled")
        out_ready = sem("out_ready")
        out_done = [sem(f"out_done{i}") for i in range(2)]

        WNAMES = "qkvo"
        NORM_LINKS = 2 * T + 1 + 2 + 3 * 3
        ROUTE_LINKS = 23

        block = ctx.enter_context(nc.Block())

        @block.sync
        def _(sp):
            sp.dma_start(c_raw[0:NB, :], c).then_inc(cond_in, 16)
            sp.dma_start(wmod_sb, wmod.rearrange("(k p) n -> p k n", p=P)).then_inc(wmod_in, 16)
            sp.dma_start(xin[:, :, :], x_t[0]).then_inc(xin_in, 16)
            sp.wait_ge(zeroed, 2)
            for m, (w, a, b) in enumerate(((wq, aq, bq), (wk, ak, bk), (wv, av, bv), (wo, ao, bo))):
                sp.dma_start(w_raw[:, m], w.rearrange("(t p) d -> p t d", p=P)).then_inc(projections_in, 16)
                sp.dma_start(a_pad[0:R, m], a).then_inc(projections_in, 16)
                sp.dma_start(b_raw[:, m], b.rearrange("(t p) r -> p t r", p=P)).then_inc(projections_in, 16)
            sp.dma_start(r_raw[0:E, :], Wg).then_inc(ffn_in, 16)
            sp.dma_start(r_raw[E:E + DH, :], A.rearrange("e r d -> (e r) d")).then_inc(expert_in, 16)
            sp.dma_start(wi_raw, Wi.rearrange("(t p) d -> p t d", p=P)).then_inc(ffn_in, 16)
            sp.dma_start(wo_raw, Wo.rearrange("(t p) f -> p t f", p=P)).then_inc(ffn_in, 16)
            for e in range(E):
                sp.dma_start(eb_raw[:, :, e * RK:(e + 1) * RK],
                             Bm[e].rearrange("(t p) r -> p t r", p=P)).then_inc(expert_in, 16)
            sp.dma_start(bg_b[:, :], bg.partition_broadcast(P)).then_inc(ffn_in, 16)

            def run(step, done, it, bank):
                kind, *a = step
                db, db_b = dense_bank(bank)
                if kind == "xin":
                    after(sp, dense_full, done("full"))
                    sp.dma_start(xin[:, :, :], x_t[(it + 2) % NB]).then_inc(xin_in, 16)
                elif kind == "xl":
                    sp.wait_ge(out_ready, done("w") + 1)
                    sp.dma_start(x1[:, :, :], x_t[it - 1]).then_inc(x1_in, 16)
                    sp.wait_ge(gates_out, 16)
                    sp.dma_start(gates_b[:, :], gates_d[it - 1].partition_broadcast(P)).then_inc(gates_in, 16)
                elif kind == "ps":
                    ot = a[0]
                    stacked = [held(sp, done(f"rs{s}") * (2 * SPLIT * 16)) for s in range(2)]
                    split = held(sp, done("pj"))
                    sp.wait_ge(part3_ready, split)
                    for s in range(2):
                        after(sp, stack_in[s], stacked[s])
                    for dst, src in ((q_d, q_part), (k_d, k_part)):
                        sp.dma_start(dst[ot], src[:, ot, :, :]).then_inc(parts_out[ot], 16)
                elif kind == "rs":
                    slot, g = a
                    ot, lower = divmod(g, 2)
                    scored, stored = held(sp, done("qk")), held(sp, done(f"ps{ot}") * (2 * 16))
                    after(sp, scores_ready, scored)
                    sp.wait_ge(parts_out[ot], stored)
                    rows = slice(lower * HG * DH, (lower + 1) * HG * DH)
                    for s in range(SPLIT):
                        for dst, src, part in ((q_st, q_d, Q_PARTS[s]), (k_st, k_d, K_PARTS[s])):
                            heads = src[ot, rows, part, :].rearrange("(j d) n -> d j n", j=HG)
                            sp.dma_start(dst[s * DH:(s + 1) * DH, slot, :, :], heads).then_inc(stack_in[slot], 16)
                elif kind == "nm":
                    sp.wait_ge(dense_free[bank], done(f"bank{bank}") + 1)
                    for j in range(HG):
                        sp.dma_start(q_st[KS:KS + 2, a[0], j, :], m_row[2 * j:2 * j + 2, :]).then_inc(m_row_in, 16)
                elif kind == "w":
                    half, t = a
                    sp.wait_ge(out_ready, done("w") + 2)
                    sp.dma_start(out_t[it - 1, 4 * half + t], ob[:, t % 2, :]).then_inc(out_done[t % 2], 16)

            walk(sp, NB, run)
            for s in out_done:
                sp.wait_ge(s, 16 * (NB * T // 2 + 1))

        @block.gpsimd
        def _(pool):
            nc.gpsimd.memset(fence[:, 0:3], 0.0).then_inc(consts_ready, 1)
            nc.gpsimd.memset(a_pad, 0.0).then_inc(zeroed, 1)
            nc.gpsimd.memset(r_raw[0:32, :], 0.0).then_inc(zeroed, 1)
            nc.gpsimd.memset(bt_pad, 0.0).then_inc(zeroed, 1)
            nc.gpsimd.memset(ident[:, :], 0.0).then_inc(zeroed, 1)
            nc.gpsimd.memset(causal_b[:, :], 0.0).then_inc(zeroed, 1)
            pool.wait_ge(zeroed, 5)
            nc.gpsimd.affine_select(out=ident[:, :], in_=ident[:, :], compare_op=ALU.not_equal, fill=1.0,
                                    base=0, pattern=[[-1, P]], channel_multiplier=1).then_inc(zeroed, 1)
            pool.wait_ge(zeroed, 6)
            nc.gpsimd.tensor_copy(ident_b[:, :], ident[:, :]).then_inc(consts_ready, 1)
            nc.gpsimd.affine_select(out=causal_b[:, :], in_=causal_b[:, :], compare_op=ALU.is_ge, fill=BIG,
                                    base=0, pattern=[[-1, P]], channel_multiplier=1).then_inc(consts_ready, 1)
            nc.gpsimd.memset(v_g[:, :, :, :, :], 0.0).then_inc(zeroed, 1)
            pool.wait_ge(zeroed, 7)
            nc.gpsimd.memset(v_g[:, :, :, :, DH:DH + 1], 1.0).then_inc(consts_ready, 1)
            for e in range(E):
                nc.gpsimd.memset(prio[:, :, e:e + 1], float(E - e)).then_inc(consts_ready, 1)

            pool.wait_ge(consts_ready, 8)
            nc.gpsimd.memset(k_st[KS:KS + 2, :, :, :], 1.0).then_inc(ones_ready, 1)
            pool.wait_ge(ones_ready, 1)
            for i in range(2):
                nc.gpsimd.memset(ob[:, i, :], 0.0).then_inc(out_done[i], 16)
            nc.gpsimd.memset(fence[:, 0:1], 0.0).then_inc(out_ready, 1)

            def run(step, done, it, bank):
                kind, *a = step
                if kind == "qk":
                    slot, ch, kt, h0, heads = a
                    if kt // 4 == ch and h0 + heads == HG:
                        par = UNITS.index((ch, kt)) % 2
                        pool.wait_ge(exp_done, done("qk") + 1)
                        after(pool, fenced, done("qk diagonal"))
                        nc.gpsimd.tensor_tensor(fence[:, 0:1], fence[:, 1:2], fence[:, 2:3],
                                                ALU.mult).then_inc(fenced, 1)
                        tri = probs[:, par, :, 0:P]
                        nc.gpsimd.affine_select(
                            out=tri, in_=tri, compare_op=ALU.is_ge, fill=0.0, base=0,
                            pattern=[[0, HG], [1, P]], channel_multiplier=-1).then_inc(masked, 1)
                elif kind == "pj":
                    which, ot, half = a
                    dst = (q_part if which == "q" else k_part)[:, ot, :, half * HB:(half + 1) * HB]
                    par = 0 if which == "q" else 1
                    pool.wait_ge(part2_ready, done("pj") + 1)
                    nc.gpsimd.tensor_tensor(dst[:, 2, :], rest[:, par, :], dst[:, 1, :],
                                            ALU.subtract).then_inc(part3_ready, 1)
                elif kind == "op":
                    i = a[0]
                    if i == 0:
                        pool.wait_ge(x1_in, 16 * (done("xl")))
                    pool.wait_ge(dense_free[bank], done(f"bank{bank}") + 1)
                    nc.gpsimd.tensor_tensor(
                        x1[:, 2 * i:2 * i + 2, :], x1[:, 2 * i:2 * i + 2, :],
                        second[:, i % 2, :].rearrange("p (t d) -> p t d", t=2), ALU.add).then_inc(x1_ready, 1)
                elif kind == "fb":
                    half, ft = a
                    pool.wait_ge(dense_free[bank], done(f"bank{bank}"))
                    nc.gpsimd.tensor_tensor(hid[:, ft, :], hid[:, ft, :], second[:, ft % 2, :],
                                            ALU.add).then_inc(hid_ready, 1)
                elif kind == "w":
                    half, t = a
                    pool.wait_ge(dense_free[bank], done(f"bank{bank}"))
                    nc.gpsimd.tensor_tensor(ob[:, t % 2, :], ob[:, t % 2, :], x1[:, 4 * half + t, :],
                                            ALU.add).then_inc(out_ready, 1)

            walk(pool, NB, run)

        @block.tensor
        def _(pe):
            def setup(i, db, db_b):
                if i == 0:
                    pe.wait_ge(consts_ready, 8)
                    pe.wait_ge(setup_chain, 3)
                    for k in range(KC):
                        last = nc.tensor.transpose(db[:, k * NB:(k + 1) * NB], c_sil[0:NB, k * P:(k + 1) * P],
                                                   ident[0:NB, 0:NB])
                elif i == 1:
                    pe.wait_ge(wmod_in, 16)
                    for n, piece in enumerate((0, 1, 2, 3, 6, 7, 8, 9)):
                        for k in range(KC):
                            last = nc.tensor.matmul(db[:, n * NB:(n + 1) * NB],
                                                    wmod_sb[:, k, piece * P:(piece + 1) * P], cond_t[:, k, :],
                                                    start=(k == 0), stop=(k == KC - 1))
                elif i == 2:
                    for n, piece in enumerate((2, 5)):
                        for k in range(KC):
                            last = nc.tensor.matmul(db[0:NB, n * D:(n + 1) * D], cond_t[:, k, :],
                                                    wmod_sb[:, k, piece * D:(piece + 1) * D],
                                                    start=(k == 0), stop=(k == KC - 1))
                elif i <= 4:
                    pe.wait_ge(projections_in, 12 * 16)
                    for n in range(2):
                        for t in range(KC):
                            last = nc.tensor.matmul(db[0:R, n * D + t * P:n * D + (t + 1) * P],
                                                    b_raw[:, 2 * (i - 3) + n, t, :], ident[:, :],
                                                    start=True, stop=True)
                elif i <= 8:
                    m = i - 5
                    for k in range(KC):
                        for t in range(KC):
                            o = db[:, k * D + t * P:k * D + (t + 1) * P]
                            nc.tensor.matmul(o, w_raw[:, m, t, k * P:(k + 1) * P], ident[:, :],
                                             start=True, stop=False)
                            last = nc.tensor.matmul(o, a_pad[:, m, k * P:(k + 1) * P],
                                                    bt_pad[:, m, t * P:(t + 1) * P], start=False, stop=True)
                elif i <= 12:
                    pe.wait_ge(ffn_in, 4 * 16)
                    pe.wait_ge(ones_ready, 1)
                    k, half = divmod(i - 9, 2)
                    for t in range(4):
                        last = nc.tensor.transpose(db[:, t * P:(t + 1) * P],
                                                   wi_raw[:, 4 * half + t, k * P:(k + 1) * P], ident[:, :])
                elif i <= 16:
                    for n in range(2):
                        for t in range(KC):
                            ft = 2 * (i - 13) + n
                            last = nc.tensor.transpose(db[:, n * D + t * P:n * D + (t + 1) * P],
                                                       wo_raw[:, t, ft * P:(ft + 1) * P], ident[:, :])
                elif i == 17:
                    pe.wait_ge(expert_in, 16 * (1 + E))
                    for k in range(KC):
                        last = nc.tensor.transpose(db[:, k * 32:(k + 1) * 32], r_raw[0:32, k * P:(k + 1) * P],
                                                   ident[0:32, 0:32])
                elif i == 18:
                    pe.wait_ge(setup_chain, 17)
                    for t in range(FT):
                        last = nc.tensor.transpose(db_b[0:KS, t * P:(t + 1) * P],
                                                   eb_w[:, t].rearrange("p s n -> p (s n)"), ident_b[:, :])
                return last

            def turned(db, f):
                for t in range(4):
                    last = nc.tensor.transpose(db[:, t * P:(t + 1) * P], f(t), ident[:, :])
                return last

            def run(step, done, it, bank):
                kind, *a = step
                db, db_b = dense_bank(bank)
                if kind == "mx":
                    slot, h0, heads, qt, chunk = a
                    n = max_keys(qt, chunk)
                    k0 = chunk * HB
                    bank_m = max_steps().index(tuple(a[1:])) % MAX_BANKS
                    after(pe, max_free, done("mx") - MAX_BANKS + 1)
                    pe.wait_ge(stack_in[slot], done(f"rs{slot}") * (2 * SPLIT * 16))
                    for j in range(heads):
                        last = nc.tensor.matmul(mxs[:, bank_m, j * n:(j + 1) * n],
                                                q_st[0:KS, slot, h0 + j, qt * P:(qt + 1) * P],
                                                k_st[0:KS, slot, h0 + j, k0:k0 + n], start=True, stop=True)
                        if qt // 4 == chunk:
                            last = nc.tensor.matmul(mxs[:, bank_m, (j + 1) * n - P:(j + 1) * n], ident_b[:, :],
                                                    causal_b[:, :], start=False, stop=True, skip_group_check=True)
                    last.then_inc(max_full, 1)
                elif kind == "qk":
                    slot, ch, kt, h0, heads = a
                    q0, n = unit_queries(ch, kt)
                    if (ch, kt, h0) == (*UNITS[0], 0):
                        pe.wait_ge(m_row_in, done("nm") * (HG * 16))
                    after(pe, exp_done, done("qk") - SCORE_BANKS + 1)
                    for j in range(heads):
                        last = nc.tensor.matmul(st[:, score_bank(ch, kt, h0), j * n:(j + 1) * n],
                                                k_st[0:KS + 2, slot, h0 + j, kt * P:(kt + 1) * P],
                                                q_st[0:KS + 2, slot, h0 + j, q0:q0 + n], start=True, stop=True)
                    last.then_inc(scores_ready, 1)
                elif kind == "pv":
                    slot, ch, kt = a
                    q0, n = unit_queries(ch, kt)
                    par = UNITS.index((ch, kt)) % 2
                    if kt == 0:
                        after(pe, ov_free, done("ov"))
                        pe.wait_ge(vg_ready, done("vg"))
                    pe.wait_ge(exp_done, done("scored") + len(score_steps(slot, ch, kt)))
                    if kt // 4 == ch:
                        pe.wait_ge(masked, done("pv diagonal") + 1)
                    for j in range(HG):
                        last = nc.tensor.matmul(ov[32 * j:32 * j + 32, HB - n:HB], v_g[:, slot, kt, j, :],
                                                probs[:, par, j, 0:n],
                                                start=(kt == 0), stop=(kt == 4 * ch + 3))
                    last.then_inc(pv_done, 1)
                elif kind == "fb":
                    half, ft = a
                    pe.wait_ge(relu_done, done("fb") + 1)
                    nc.tensor.matmul(db[:, :], b_stack[0:KS, ft * P:(ft + 1) * P],
                                     low_st[0:KS, 1, half * HB:(half + 1) * HB], start=False, stop=True,
                                     skip_group_check=True).then_inc(dense_full, 1)
                elif kind == "w":
                    half, t = a
                    for ft in range(FT // 2, FT):
                        if t == 0 and ft in (FT // 2, FT - 2):
                            pe.wait_ge(hid_ready, done("fb") - (2 if ft < FT - 2 else 0))
                        last = nc.tensor.matmul(db[:, 0:D], hid[:, ft, t * P:(t + 1) * P], wo_t[:, ft, :],
                                                start=False, stop=(ft == FT - 1))
                    last.then_inc(dense_full, 1)
                elif kind in DENSE:
                    if step[0:2] in (("su", 1), ("su", 5), ("ct", 0), ("op", 0)) or kind in ("rt", "rx") or step in (
                            ("pj", "q", 0, 0), ("fa", 0, 0)):
                        evacuated(pe, done)
                    else:
                        after(pe, dense_free[bank], done(f"bank{bank}"))
                    if kind == "su":
                        last = setup(a[0], db, db_b)
                    elif kind == "t1":
                        k, half = divmod(a[0], 2)
                        pe.wait_ge(norm1_ready, done("ln1"))
                        last = turned(db, lambda t: xin[:, 4 * half + t, k * P:(k + 1) * P])
                    elif kind == "t2":
                        k, half = divmod(a[0], 2)
                        pe.wait_ge(norm2_ready, done("ln2"))
                        last = turned(db, lambda t: x2n[:, 4 * half + t, k * P:(k + 1) * P])
                    elif kind == "ct":
                        k, half = divmod(a[0], 2)
                        last = turned(db, lambda t: ctx_n[:, 4 * half + t, k * P:(k + 1) * P])
                    elif kind == "ce":
                        pe.wait_ge(ov_free, done("ov"))
                        last = turned(db, lambda t: o_sb[:, a[1], t * P:(t + 1) * P])
                    elif kind == "rb":
                        pe.wait_ge(route_ready, done("ro"))
                        last = turned(db, lambda t: ratio_w[:, 4 * a[0] + t, :])
                    elif kind == "mt":
                        pe.wait_ge(route_ready, done("ro"))
                        for t in range(T):
                            last = nc.tensor.transpose(db_b[0:KS, t * P:(t + 1) * P],
                                                       low_w[:, a[0], t].rearrange("p s n -> p (s n)"), ident_b[:, :])
                    elif kind == "nm":
                        pe.wait_ge(negm_split, done("ms"))
                        for t in range(T):
                            last = nc.tensor.transpose(db_b[0:2 * HG, t * P:(t + 1) * P],
                                                       m_w[:, t].rearrange("p j s -> p (j s)"), ident_b[:, :])
                    elif kind == "pj":
                        which, ot, half = a
                        for k in range(KC):
                            last = nc.tensor.matmul(db[:, :], w_t[:, WNAMES.index(which), k, ot * P:(ot + 1) * P],
                                                    h_t[:, k, half * HB:(half + 1) * HB],
                                                    start=(k == 0), stop=(k == KC - 1))
                    elif kind in ("vp", "op"):
                        src, m = (h_t, 2) if kind == "vp" else (c_t, 3)
                        for n in range(2):
                            t = 2 * a[0] + n
                            for k in range(KC):
                                last = nc.tensor.matmul(db[:, n * D:(n + 1) * D], src[:, k, t * P:(t + 1) * P],
                                                        w_t[:, m, k, :], start=(k == 0), stop=(k == KC - 1))
                    elif kind == "rt":
                        for k in range(KC):
                            for j in range(4):
                                last = nc.tensor.matmul(db[32 * j:32 * j + 32, 0:D], rout_t[:, k, :],
                                                        c_t[:, k, j * D:(j + 1) * D],
                                                        start=(k == 0), stop=(k == KC - 1))
                    elif kind == "rx":
                        for s in range(2):
                            last = nc.tensor.transpose(db[:, s * P:(s + 1) * P], rout_sb[:, s * P:(s + 1) * P],
                                                       ident[:, :])
                    elif kind == "fa":
                        half, ft = a
                        for k in range(KC):
                            nc.tensor.matmul(db[:, :], wi_t[:, k, ft * P:(ft + 1) * P],
                                             c_t[:, k, half * HB:(half + 1) * HB], start=(k == 0), stop=False)
                        last = nc.tensor.matmul(db[:, :], b_stack[0:KS, ft * P:(ft + 1) * P],
                                                low_st[0:KS, 0, half * HB:(half + 1) * HB], start=False, stop=True)
                        last.then_inc(base_full, 1)
                        return
                    elif kind == "wa":
                        half, t = a
                        for ft in range(FT // 2):
                            if (t, ft) == (0, 0):
                                pe.wait_ge(hid_ready, done("fb") - FT // 2)
                            nc.tensor.matmul(db[:, 0:D], hid[:, ft, t * P:(t + 1) * P], wo_t[:, ft, :],
                                             start=(ft == 0), stop=False)
                        return
                    last.then_inc(dense_full, 1)

            walk(pe, NB, run)

        @block.scalar
        def _(act):
            def setup(i, db, db_b, done):
                if i == 0:
                    act.wait_ge(cond_in, 16)
                    nc.scalar.activation(c_sig[0:NB, :], c_raw[0:NB, :], ACT.Exp, scale=-1.0).then_inc(cond_exp, 1)
                act.wait_ge(dense_full, done("full") + 1)
                if i == 0:
                    return nc.scalar.copy(cond_t, db[:, 0:KC * NB].rearrange("p (k b) -> p k b", k=KC))
                if i == 1:
                    return nc.scalar.copy(mod_t[:, :, :].rearrange("p b n -> p n b"),
                                          db[:, 0:8 * NB].rearrange("p (n b) -> p n b", b=NB))
                if i == 2:
                    return nc.scalar.copy(gate_raw[0:NB, :], db[0:NB, :])
                if i <= 4:
                    return nc.scalar.mul(bt_pad[0:R, 2 * (i - 3):2 * (i - 3) + 2, :],
                                         db[0:R, :].rearrange("p (m d) -> p m d", m=2), LORA_SCALE)
                if i <= 8:
                    return nc.scalar.copy(w_t[:, i - 5, :, :], db[:, :].rearrange("p (k d) -> p k d", k=KC))
                if i <= 12:
                    k, half = divmod(i - 9, 2)
                    return nc.scalar.copy(wi_t[:, k, half * HB:(half + 1) * HB], db[:, :])
                if i <= 16:
                    return nc.scalar.copy(wo_t[:, 2 * (i - 13):2 * (i - 13) + 2, :],
                                          db[:, :].rearrange("p (k d) -> p k d", k=2))
                if i == 17:
                    return nc.scalar.copy(rout_t[:, :, :], db[:, 0:KC * 32].rearrange("p (k n) -> p k n", k=KC))
                if i == 18:
                    return nc.scalar.copy(b_stack[0:KS, :], db_b[0:KS, :])

            def run(step, done, it, bank):
                kind, *a = step
                db, db_b = dense_bank(bank)
                if kind == "qk":
                    slot, ch, kt, h0, heads = a
                    n = unit_queries(ch, kt)[1]
                    par = UNITS.index((ch, kt)) % 2
                    if h0 == 0:
                        after(act, pv_done, done("pv"))
                    act.wait_ge(scores_ready, done("qk") + 1)
                    nc.scalar.activation(probs[:, par, h0:h0 + heads, 0:n],
                                         st[:, score_bank(ch, kt, h0), 0:heads * n].rearrange("p (j q) -> p j q", q=n),
                                         ACT.Exp, scale=SCORE_SCALE).then_inc(exp_done, 1)
                    return
                if kind == "ov":
                    act.wait_ge(pv_done, done("pv"))
                    nc.scalar.copy(o_sb[:, a[0], :], ov[:, :]).then_inc(ov_free, 1)
                    return
                if kind == "ro":
                    act.wait_ge(route_diff, done("ro") + 1)
                    nc.scalar.activation(rv[:, 1], rv[:, 0], ACT.Exp).then_inc(route_exp, 1)
                    return
                if kind == "su":
                    setup(a[0], db, db_b, done).then_inc(dense_free[bank], 1)
                    if a[0] == 5:
                        act.wait_ge(setup_chain, 10)
                        act.dma_start(gates_d, gate_raw[0:NB, :]).then_inc(gates_out, 16)
                    return
                if kind not in ("t1", "t2", "pj", "vp", "ct", "rt", "mt", "rb", "fa", "nm"):
                    return
                if kind == "fa":
                    half, ft = a
                    act.wait_ge(base_full, done("fa") + 1)
                    nc.scalar.activation(hid[:, ft, :], db[:, :], ACT.Relu).then_inc(relu_done, 1)
                    return
                act.wait_ge(dense_full, done("full") + 1)
                if kind in ("t1", "t2"):
                    k, half = divmod(a[0], 2)
                    dst, mod = (h_t, mod1) if kind == "t1" else (c_t, mod2)
                    nc.scalar.activation(dst[:, k, half * HB:(half + 1) * HB], db[:, :], ACT.Identity,
                                         scale=mod[:, 2 + k:3 + k], bias=mod[:, k:k + 1]).then_inc(dense_free[bank], 1)
                elif kind == "pj":
                    which, ot, half = a
                    dst = (q_part if which == "q" else k_part)[:, ot, :, half * HB:(half + 1) * HB]
                    if isinstance(it, int) and it < 0:
                        act.wait_ge(gates_out, 16)
                    after(act, parts_out[ot], done(f"ps{ot}") * (2 * 16))
                    nc.scalar.copy(dst[:, 0, :], db[:, :]).then_inc(part1_ready, 1)
                elif kind == "vp":
                    after(act, vg_ready, done("vg"))
                    nc.scalar.copy(v_st[:, 2 * a[0]:2 * a[0] + 2, :],
                                   db[:, :].rearrange("p (t d) -> p t d", t=2)).then_inc(dense_free[bank], 1)
                elif kind == "ct":
                    k, half = divmod(a[0], 2)
                    nc.scalar.copy(c_t[:, k, half * HB:(half + 1) * HB], db[:, :]).then_inc(dense_free[bank], 1)
                elif kind == "rt":
                    nc.scalar.copy(rout_sb[:, :], db[:, 0:D]).then_inc(dense_free[bank], 1)
                elif kind == "mt":
                    nc.scalar.copy(low_st[0:KS, a[0], :], db_b[0:KS, :]).then_inc(dense_free[bank], 1)
                elif kind == "rb":
                    nc.scalar.copy(ratio_b[:, a[0], :], db[:, :]).then_inc(dense_free[bank], 1)
                elif kind == "nm":
                    nc.scalar.copy(m_row[:, :], db_b[0:2 * HG, :]).then_inc(dense_free[bank], 1)

            walk(act, NB, run)

        @block.vector
        def _(dve):
            links = {"setup": 0}

            def setup_link(ins):
                links["setup"] += 1
                ins.then_inc(setup_chain, 1)
                dve.wait_ge(setup_chain, links["setup"])

            def setup_before():
                dve.wait_ge(cond_exp, 1)
                setup_link(nc.vector.tensor_scalar_add(c_sig[0:NB, :], c_sig[0:NB, :], 1.0))
                setup_link(nc.vector.reciprocal(c_sig[0:NB, :], c_sig[0:NB, :]))
                setup_link(nc.vector.tensor_tensor(c_sil[0:NB, :], c_sig[0:NB, :], c_raw[0:NB, :], ALU.mult))
                setup_link(nc.vector.memset(negm[:, :, :], 0.0))

            def setup_expert():
                dve.wait_ge(expert_in, 16 * (1 + E))
                setup_link(nc.vector.tensor_copy(eb_w[:, :, 0, :], eb_raw))
                setup_link(nc.vector.tensor_tensor(eb_rest, eb_raw, eb_w[:, :, 0, :], ALU.subtract))
                setup_link(nc.vector.tensor_copy(eb_w[:, :, 1, :], eb_rest))
                setup_link(nc.vector.tensor_tensor(eb_w[:, :, 4, :], eb_rest, eb_w[:, :, 1, :], ALU.subtract))
                setup_link(nc.vector.tensor_copy(eb_w[:, :, 2, :], eb_w[:, :, 0, :]))
                setup_link(nc.vector.tensor_copy(eb_w[:, :, 3, :], eb_w[:, :, 1, :]))
                setup_link(nc.vector.tensor_copy(eb_w[:, :, 5, :], eb_w[:, :, 0, :]))

            def setup_gates():
                dve.wait_ge(dense_free[0], 2)
                dve.wait_ge(dense_free[1], 1)
                setup_link(nc.vector.tensor_scalar_add(mod_t[:, :, 2:4], mod_t[:, :, 2:4], 1.0))
                setup_link(nc.vector.tensor_scalar_add(mod_t[:, :, 6:8], mod_t[:, :, 6:8], 1.0))
                setup_link(nc.vector.tensor_scalar(gate_sgn[0:NB, :], gate_raw[0:NB, :], 0.0, 2.0,
                                                   ALU.is_ge, ALU.mult))
                setup_link(nc.vector.scalar_tensor_tensor(
                    out=gate_abs[0:NB, :], in0=gate_raw[0:NB, :], scalar=-1.0, in1=gate_raw[0:NB, :],
                    op0=ALU.mult, op1=ALU.max))
                setup_link(nc.vector.tensor_scalar(gate_abs[0:NB, :], gate_abs[0:NB, :], GATE_MIN, None, ALU.max))
                setup_link(nc.vector.scalar_tensor_tensor(
                    out=gate_raw[0:NB, :], in0=gate_sgn[0:NB, :], scalar=-1.0, in1=gate_abs[0:NB, :],
                    op0=ALU.add, op1=ALU.mult))

            def norm_stats(src, n):
                links = n * NORM_LINKS
                for t in range(T):
                    nc.vector.bn_stats(stats[:, t, :], src[:, t, :]).then_inc(norm_chain, 1)
                dve.wait_ge(norm_chain, links + T)
                nc.vector.memset(fence[:, 3:4], 0.0)
                for t in range(T):
                    nc.vector.bn_aggr(mv[:, t, :], stats[:, t, :]).then_inc(norm_chain, 1)

            def normalise(src, dst, n, ready):
                k = [2 * T]

                def link(ins):
                    k[0] += 1
                    ins.then_inc(norm_chain, 1)
                    dve.wait_ge(norm_chain, n * NORM_LINKS + k[0])

                dve.wait_ge(norm_chain, n * NORM_LINKS + k[0])
                var, y, b, sq = (nt[:, i, :] for i in range(4))
                link(nc.vector.tensor_scalar_add(var, mv[:, :, 1], LN_EPS))
                link(nc.vector.tensor_scalar(b.bitcast(I32), var.bitcast(I32), 1, None, ALU.arith_shift_right))
                link(nc.vector.tensor_scalar(y.bitcast(I32), b.bitcast(I32), -1.0, RSQRT_SEED, ALU.mult, ALU.add))
                for _ in range(3):
                    link(nc.vector.tensor_tensor(sq, y, y, ALU.mult))
                    link(nc.vector.scalar_tensor_tensor(out=b, in0=sq, scalar=-0.5, in1=var, op0=ALU.mult,
                                                        op1=ALU.mult))
                    link(nc.vector.scalar_tensor_tensor(out=y, in0=b, scalar=1.5, in1=y, op0=ALU.add,
                                                        op1=ALU.mult))
                assert k[0] == NORM_LINKS
                for t in range(T):
                    last = nc.vector.tensor_scalar(dst[:, t, :], src[:, t, :], mv[:, t, 0:1], y[:, t:t + 1],
                                                   ALU.subtract, ALU.mult)
                last.then_inc(ready, 1)

            def route(n, it):
                k = [0]

                def link(ins):
                    k[0] += 1
                    ins.then_inc(route_chain, 1)
                    dve.wait_ge(route_chain, n * ROUTE_LINKS + k[0])

                d, ex, v, sel1, d2, v2, sel2, wt = (rv[:, i] for i in range(8))
                top, s1, m2, s2, total, w1, r = (rs_[:, i] for i in range(7))

                def wide(s):
                    return s.unsqueeze(2).broadcast_to([P, T, E])

                link(nc.vector.tensor_tensor(wt, lg[:, :, 0:E], bg_b[:, :].unsqueeze(1).broadcast_to([P, T, E]),
                                             ALU.add))
                link(nc.vector.tensor_reduce(top, wt, axis=AX.X, op=ALU.max))
                nc.vector.tensor_tensor(d, wt, wide(top), ALU.subtract).then_inc(route_diff, 1)
                dve.wait_ge(route_diff, n + 1)
                link(nc.vector.scalar_tensor_tensor(out=v, in0=d, scalar=0.0, in1=prio[:, :, :],
                                                    op0=ALU.is_equal, op1=ALU.mult))
                link(nc.vector.tensor_reduce(s1, v, axis=AX.X, op=ALU.max))
                link(nc.vector.tensor_tensor(sel1, v, wide(s1), ALU.is_equal))
                link(nc.vector.scalar_tensor_tensor(out=d2, in0=sel1, scalar=BIG, in1=d, op0=ALU.mult, op1=ALU.add))
                link(nc.vector.tensor_reduce(m2, d2, axis=AX.X, op=ALU.max))
                link(nc.vector.tensor_tensor(d2, d2, wide(m2), ALU.subtract))
                link(nc.vector.scalar_tensor_tensor(out=v2, in0=d2, scalar=0.0, in1=prio[:, :, :],
                                                    op0=ALU.is_equal, op1=ALU.mult))
                link(nc.vector.tensor_reduce(s2, v2, axis=AX.X, op=ALU.max))
                link(nc.vector.tensor_tensor(sel2, v2, wide(s2), ALU.is_equal))
                dve.wait_ge(route_exp, n + 1)
                link(nc.vector.tensor_reduce(total, ex, axis=AX.X, op=ALU.add))
                link(nc.vector.reciprocal(w1, total))
                link(nc.vector.tensor_tensor(wt, ex, sel2, ALU.mult))
                link(nc.vector.tensor_reduce(r, wt, axis=AX.X, op=ALU.add))
                link(nc.vector.tensor_copy(ratio_w[:, :, :], r.unsqueeze(2).broadcast_to([P, T, P])))
                link(nc.vector.tensor_tensor(d2, sel2, sel1, ALU.subtract))
                low = lg[:, :, E:E + DH].rearrange("p t (e r) -> p t e r", e=E)
                for i, mask in enumerate((sel1, d2)):
                    last = nc.vector.tensor_tensor(
                        lowf[:, i].rearrange("p t (e r) -> p t e r", e=E), low,
                        mask.unsqueeze(3).broadcast_to([P, T, E, RK]), ALU.mult)
                    if i == 0:
                        k[0] += 1
                        last.then_inc(route_chain, 1)
                link(last)
                full = lowf[:, :, :, :].rearrange("p v t n -> p (v t) n")
                left = lowr[:, :, :, :].rearrange("p v t n -> p (v t) n")
                stack = low_w[:, :, :, :, :].rearrange("p v t s n -> p (v t) s n")
                nvt = 2 * T
                link(nc.vector.tensor_copy(stack[:, :, 0:2, :], full.unsqueeze(2).broadcast_to([P, nvt, 2, DH])))
                nc.vector.tensor_copy(stack[:, :, 4, :], full).then_inc(route_chain, 1)
                k[0] += 1
                link(nc.vector.tensor_tensor(left, full, stack[:, :, 0, :], ALU.subtract))
                link(nc.vector.tensor_copy(stack[:, :, 2:4, :], left.unsqueeze(2).broadcast_to([P, nvt, 2, DH])))
                assert k[0] == ROUTE_LINKS, k[0]
                nc.vector.tensor_tensor(stack[:, :, 5, :], left, stack[:, :, 2, :],
                                        ALU.subtract).then_inc(route_ready, 1)

            def run(step, done, it, bank):
                kind, *a = step
                db, db_b = dense_bank(bank)
                if kind == "su":
                    if a[0] == 0:
                        setup_before()
                    elif a[0] == 3:
                        setup_gates()
                        dve.wait_ge(consts_ready, 8)
                    elif a[0] == N_PROJECTION_SETUP:
                        setup_expert()
                elif kind == "ls1":
                    dve.wait_ge(xin_in, 16 * (done("ls1") + 1))
                    norm_stats(xin, done("ls1") + done("ls2"))
                elif kind == "ln1":
                    nc.vector.tensor_copy(mod1[:, :], mod_t[:, it + 1, 0:4] if isinstance(it, int)
                                          else mod_t[:, bass.ds(it + 1, 1), 0:4].rearrange("p b n -> p (b n)"))
                    normalise(xin, xin, done("ln1") + done("ln2"), norm1_ready)
                elif kind == "ls2":
                    dve.wait_ge(x1_ready, done("op"))
                    norm_stats(x1, done("ls1") + done("ls2"))
                elif kind == "ln2":
                    nc.vector.tensor_copy(mod2[:, :], mod_t[:, it - 1, 4:8] if isinstance(it, int)
                                          else mod_t[:, bass.ds(it - 1, 1), 4:8].rearrange("p b n -> p (b n)"))
                    normalise(x1, x2n, done("ln1") + done("ln2"), norm2_ready)
                elif kind == "ro":
                    evacuated(dve, done)
                    route(done("ro"), it)
                elif kind == "mx":
                    slot, h0, heads, qt, chunk = a
                    n = max_keys(qt, chunk)
                    dve.wait_ge(max_full, done("mx") + 1)
                    src = mxs[:, max_steps().index(tuple(a[1:])) % MAX_BANKS, 0:heads * n].rearrange("p (j k) -> p j k", k=n)
                    dst = negm[:, qt] if chunk == qt // 4 else negm_left[:, qt - 4]
                    nc.vector.tensor_reduce(dst[:, h0:h0 + heads], src, axis=AX.X, op=ALU.max,
                                            negate=True).then_inc(max_free, 1)
                elif kind == "vg":
                    g = a[0]
                    if g == 0:
                        evacuated(dve, done)
                    after(dve, pv_done, done("pv") - VG_UNIT - 1)
                    nc.vector.tensor_copy(
                        v_g[:, g % 2, :, :, 0:DH],
                        v_st[:, :, HG * DH * g:HG * DH * (g + 1)].rearrange("p t (j d) -> p t j d", j=HG)
                    ).then_inc(vg_ready, 1)
                elif kind == "ms":
                    dve.wait_ge(max_free, done("mx"))
                    nc.vector.tensor_tensor(negm[:, 4:T, :], negm[:, 4:T, :], negm_left[:, :, :],
                                            ALU.min).then_inc(negm_ready, 1)
                    dve.wait_ge(negm_ready, done("ms") + 1)
                    nc.vector.tensor_copy(m_w[:, :, :, 0], negm[:, :, :]).then_inc(negm_hi, 1)
                    dve.wait_ge(negm_hi, done("ms") + 1)
                    nc.vector.tensor_tensor(m_w[:, :, :, 1], negm[:, :, :], m_w[:, :, :, 0],
                                            ALU.subtract).then_inc(negm_split, 1)
                elif kind == "pj":
                    which, ot, half = a
                    dst = (q_part if which == "q" else k_part)[:, ot, :, half * HB:(half + 1) * HB]
                    par = 0 if which == "q" else 1
                    dve.wait_ge(part1_ready, done("pj") + 1)
                    after(dve, part3_ready, done("pj") - 1)
                    nc.vector.tensor_tensor(rest[:, par, :], db[:, :], dst[:, 0, :],
                                            ALU.subtract).then_inc(dense_free[bank], 1)
                    dve.wait_ge(dense_free[bank], done(f"bank{bank}") + 1)
                    nc.vector.tensor_copy(dst[:, 1, :], rest[:, par, :]).then_inc(part2_ready, 1)
                elif kind == "ce":
                    g, ch = a
                    dve.wait_ge(dense_full, done("full") + 1)
                    o = db[:, :].rearrange("p (q j e) -> p q j e", q=4, j=HG)
                    nc.vector.reciprocal(rsum[:, :, :], o[:, :, :, DH]).then_inc(rsum_ready, 1)
                    dve.wait_ge(rsum_ready, done("ce") + 1)
                    nc.vector.tensor_tensor(
                        ctx_n[:, 4 * ch:4 * ch + 4, HG * DH * g:HG * DH * (g + 1)].rearrange(
                            "p q (j d) -> p q j d", j=HG),
                        o[:, :, :, 0:DH], rsum[:, :, :].unsqueeze(3).broadcast_to([P, 4, HG, DH]),
                        ALU.mult).then_inc(dense_free[bank], 1)
                elif kind == "op":
                    i = a[0]
                    if i == 0:
                        dve.wait_ge(gates_in, 16 * done("xl"))
                    dve.wait_ge(dense_full, done("full") + 1)
                    if i >= 2:
                        dve.wait_ge(x1_ready, done("op") - 1)
                    nc.vector.tensor_tensor(
                        second[:, i % 2, :].rearrange("p (t d) -> p t d", t=2),
                        db[:, :].rearrange("p (t d) -> p t d", t=2),
                        gates_b[:, 0:D].unsqueeze(1).broadcast_to([P, 2, D]), ALU.mult).then_inc(dense_free[bank], 1)
                elif kind == "rx":
                    dve.wait_ge(dense_full, done("full") + 1)
                    for s in range(2):
                        last = nc.vector.tensor_copy(
                            lg[:, :, :].rearrange("p (j s) n -> p s j n", s=2)[:, s],
                            db[:, s * P:(s + 1) * P].rearrange("p (j n) -> p j n", j=4)[:, :, 0:E + DH])
                    last.then_inc(dense_free[bank], 1)
                elif kind == "fb":
                    half, ft = a
                    dve.wait_ge(dense_full, done("full") + 1)
                    if (half, ft) >= (0, 2):
                        dve.wait_ge(hid_ready, done("fb") - 1)
                    nc.vector.scalar_tensor_tensor(out=second[:, ft % 2, :], in0=db[:, :], scalar=0.0,
                                                   in1=ratio_b[:, half, :], op0=ALU.max,
                                                   op1=ALU.mult).then_inc(dense_free[bank], 1)
                elif kind == "w":
                    half, t = a
                    dve.wait_ge(dense_full, done("full") + 1)
                    dve.wait_ge(out_done[t % 2], 16 * (done(f"w{t % 2}") + 1))
                    nc.vector.scalar_tensor_tensor(out=ob[:, t % 2, :], in0=db[:, 0:D],
                                                   scalar=rs_[:, 5, 4 * half + t:4 * half + t + 1],
                                                   in1=gates_b[:, D:2 * D], op0=ALU.mult,
                                                   op1=ALU.mult).then_inc(dense_free[bank], 1)

            walk(dve, NB, run, late="pj")


_INS = ["L0_attn_x", "L0_attn_wq", "L0_attn_aq", "L0_attn_bq", "L0_attn_wk", "L0_attn_ak", "L0_attn_bk",
        "L0_attn_wv", "L0_attn_av", "L0_attn_bv", "L0_attn_wo", "L0_attn_ao", "L0_attn_bo", "L0_ffn_Wg",
        "L0_ffn_bg", "L0_ffn_Wi", "L0_ffn_Wo", "L0_ffn_A", "L0_ffn_B", "L0_c", "L0_wmod"]


def kernel(**inputs):
    import numpy as np
    import concourse.bacc as bacc
    from concourse.bass_utils import run_bass_kernel_spmd

    nc = bacc.Bacc("TRN2", target_bir_lowering=False, num_devices=1)
    arrays, args = {}, []
    for name in _INS:
        a = np.ascontiguousarray(inputs[name])
        arrays[f"in_{name}"] = a
        args.append(nc.dram_tensor(f"in_{name}", a.shape, mybir.dt.from_np(a.dtype), kind="ExternalInput").ap())
    x = inputs["L0_attn_x"]
    args.append(nc.dram_tensor("out_x", x.shape, F32, kind="ExternalOutput").ap())
    adaln_block(nc, *args)
    r = run_bass_kernel_spmd(nc, [arrays], core_ids=[0])
    return r.results[0]["out_x"]
```
